# Optimizing a Trainium2 kernel written in Bass

```python
import numpy as np
import jax
import jax.numpy as jnp

def _softmax(x, axis=-1):
    return jax.nn.softmax(x, axis=axis)
def _gelu(x):
    return jax.nn.gelu(x, approximate=True)
def _silu(x):
    return jax.nn.silu(x)
def _sigmoid(x):
    return jax.nn.sigmoid(x)
def _layernorm(x, axis=-1, eps=1e-5):
    m = jnp.mean(x, axis=axis, keepdims=True)
    v = jnp.var(x, axis=axis, keepdims=True)
    return (x - m) / jnp.sqrt(v + eps)
def _scatter_add(tgt, idx, src, axis=0):
    return tgt.at[idx].add(src)
def _segment_sum(src, seg, n):
    return jax.ops.segment_sum(src, seg, n)

kernel_name = 'mk_adj_preln_d1_adj_128_10e8f1'

def setup_inputs(seed: int = 0):
    np.random.seed(seed)
    _w = jnp.asarray
    def _rec_inputs():
        import jax
        import jax.numpy as jnp
        _gk = jax.random.key(seed)
        x = -0.000929 + 1 * jax.random.normal(jax.random.fold_in(_gk, 1), (8192, 128), jnp.float32)
        _a = jax.random.bernoulli(jax.random.fold_in(_gk, 2), 0.000488281, (8192, 8192))
        adj = _a.astype(jnp.int32)
        return x, adj
    x, adj = _rec_inputs()
    def _L0_gnn_setup():
        import jax, jax.numpy as jnp
        import numpy as np
        NEG_INF = -9000000000000000.0
        ALPHA = 0.2
        key = jax.random.key(seed)
        k1, k2, k3, k4 = jax.random.split(key, 4)
        N, F_in, F_out = (8192, 128, 128)
        x = jax.random.normal(k1, (N, F_in), dtype=jnp.float32)
        adj = jax.random.randint(k2, (N, N), 0, 2, dtype=jnp.int32)
        W = jax.random.normal(k3, (F_in, F_out), dtype=jnp.float32) * (1.0 / np.sqrt(F_in))
        a = jax.random.normal(k4, (2 * F_out, 1), dtype=jnp.float32) * (1.0 / np.sqrt(2 * F_out))
        return {'x': x, 'adj': adj, 'W': W, 'a': a}
    _L0_gnn_all = _L0_gnn_setup()
    _L0_gnn_in = {k: v for k, v in _L0_gnn_all.items() if k in ('W', 'a', )}
    del _L0_gnn_all

    return {
        "x": x,
        "adj": adj,
        "L0_gnn_W": _L0_gnn_in["W"],
        "L0_gnn_a": _L0_gnn_in["a"],
    }

def reference(x, adj, L0_gnn_W, L0_gnn_a):
    import jax
    import jax.numpy as jnp
    def _L0_gnn_ref(x, adj, W, a):
        import jax, jax.numpy as jnp
        import numpy as np
        NEG_INF = -9000000000000000.0
        ALPHA = 0.2
        h = x @ W
        F_out = h.shape[1]
        a_src = a[:F_out, 0]
        a_dst = a[F_out:, 0]
        s_src = h @ a_src
        s_dst = h @ a_dst
        e = jax.nn.leaky_relu(s_src[:, None] + s_dst[None, :], negative_slope=ALPHA)
        e = jnp.where(adj > 0, e, jnp.float32(NEG_INF))
        attention = jax.nn.softmax(e, axis=1)
        h_prime = attention @ h
        return h_prime

    h = jnp.maximum(_layernorm(x, axis=-1), 0.0)
    x = x + _L0_gnn_ref(h, adj, L0_gnn_W, L0_gnn_a)
    return x


_drawn_inputs = setup_inputs


def setup_inputs(seed=0):
    import zlib

    import numpy as np

    out = dict(_drawn_inputs(seed))
    spreads = {}
    factors = {}
    for name, (base, spread) in spreads.items():
        noise = np.random.default_rng([zlib.crc32(name.encode()), seed]).standard_normal(out[name].shape)
        drawn = base * np.exp(spread * noise) if base else spread * noise
        out[name] = jnp.asarray(drawn.astype(out[name].dtype))
    for name, factor in factors.items():
        out[name] = (out[name] * factor).astype(out[name].dtype)
    return out
```

```python
import concourse.bass as bass
from concourse import mybir
from contextlib import ExitStack

P = 128
N = 8192
F = 128
TILES = N // P
QUARTER = TILES // 4
BATCH = 4
BATCHES = TILES // BATCH
GROUPS = 2
GROUP_BATCHES = BATCHES // GROUPS
BIT_COLS = 512
BITS = N // BIT_COLS
HALVES = 2
HALF = N // HALVES
HALF_BITS = BITS // HALVES
AHEAD = 5
SLOTS = 8
WIDE = 16
ROW = F + 2
S_COL, D_COL = F, F + 1
REC = WIDE + 4
REC_S, REC_NODE, REC_ONE = WIDE, WIDE + 1, WIDE + 2
EPS = 1e-5
ALPHA = 0.2
MASKED = 9e15
EXP_BIAS = 127 * BIT_COLS
DVE_STEPS = 100
SKIP = 100000.0


class Count:

    def __init__(self, sem, credit=0):
        self.sem, self.base, self.n, self.total = sem, credit, 0, credit

    def add(self, ins):
        ins.then_inc(self.sem, 1)
        self.n += 1
        return self.value()

    def value(self):
        return self.base + self.n

    def enter(self, i, per):
        self.total += self.n
        self.base, self.n, self.per = i * per + self.total, 0, per

    def leave(self, times):
        assert self.n == self.per, f"{self.n} signals in the loop's body, not {self.per}"
        self.total += times * self.per
        self.base, self.n = self.total, 0


def gat_kernel(nc, x, adj, W, a, out):
    f32, bf16 = mybir.dt.float32, mybir.dt.bfloat16
    i32, u32 = mybir.dt.int32, mybir.dt.uint32
    ALU, ACT, AX = mybir.AluOpType, mybir.ActivationFunctionType, mybir.AxisListType

    table = nc.dram_tensor("table", (N, ROW), f32).ap()

    ctx = ExitStack()
    with ctx:
        def sb(name, shape, dt):
            return ctx.enter_context(nc.sbuf_tensor(name, shape, dt))

        def sem(name):
            return ctx.enter_context(nc.semaphore(name))

        adj_buf = sb("adj_buf", [P, BATCH * HALVES, HALF], i32)
        gathered = sb("gathered", [P, 2, BATCH * SLOTS * ROW], f32)
        mask_buf = sb("mask_buf", [P, HALVES, HALF], bf16)
        x_all = gathered[:, :, :].rearrange("p a n -> p (a n)")[:, 0:N].rearrange("p (t f) -> p t f", f=F)
        g_view = [gathered[:, par, :].rearrange("p (b k n) -> p b k n", b=BATCH, k=SLOTS) for par in (0, 1)]
        work = mask_buf[:, :, :].rearrange("p h n -> p (h n)").bitcast(f32)
        normed = [work[:, 512 * k:512 * k + 512].rearrange("p (b f) -> p b f", b=BATCH) for k in (0, 1)]
        relu_t = [work[:, 1024 + 512 * k:1536 + 512 * k].rearrange("p (b f) -> p b f", b=BATCH) for k in (0, 1)]
        rows = [work[:, 2048 + 1024 * k:2048 + 1024 * k + BATCH * ROW].rearrange("p (b n) -> p b n", b=BATCH) for k in (0, 1)]
        e_blk, p_t = normed[0], relu_t[0]
        h_blk = work[:, 2048:2560].rearrange("p (b f) -> p b f", b=BATCH)
        x_row, o_row, d_diag = normed[1][:, 0, :], normed[1][:, 1, :], normed[1][:, 2, :]
        flat = adj_buf[:, :, :].rearrange("p u n -> p (u n)")
        dense_adj = flat[:, 0:N]
        dense_d = flat[:, N:2 * N].bitcast(f32)
        dense_e = flat[:, 2 * N:3 * N].bitcast(f32)
        dense_m = flat[:, 3 * N:4 * N].bitcast(f32)

        w_ext = sb("w_ext", [P, ROW], f32)
        a_sb = sb("a_sb", [P, 2], f32)
        column_1 = sb("column_1", [P, P], f32)
        node0 = sb("node0", [P, BATCH], i32)
        ident = sb("ident", [P, P], f32)
        ones = sb("ones", [P, P], f32)
        ones_b = sb("ones_b", [P, P], bf16)
        before = sb("before", [P, P], bf16)
        bit_ident = sb("bit_ident", [P, HALF_BITS, P], bf16)
        key_rows = sb("key_rows", [P, BIT_COLS], bf16)
        stats = sb("stats", [P, QUARTER // 2, 6], f32)
        mv_all = sb("mv_all", [P, TILES, 2], f32)
        std = sb("std", [P, TILES], f32)
        rstd = sb("rstd", [P, TILES], f32)
        newton = sb("newton", [P, QUARTER], f32)
        eps = sb("eps", [P, 1], f32)
        var_e = sb("var_e", [P, TILES], f32)
        mean_h = sb("mean_h", [P, F], f32)
        sd_all = sb("sd_all", [P, TILES, 2], f32)
        fence = sb("fence", [P, 1], f32)
        pool_fence = sb("pool_fence", [P, 1], f32)
        rest = sb("rest", [P, BIT_COLS], f32)
        words = sb("words", [P, BATCH, WIDE], f32)
        wi = [sb(f"wi{k}", [P, BATCH, WIDE], i32) for k in range(3)]
        wf = [sb(f"wf{k}", [P, BATCH, WIDE], f32) for k in range(3)]
        top_bit = sb("top_bit", [P, BATCH, WIDE], i32)
        cand = sb("cand", [P, BATCH, 2 * WIDE], f32)
        cand_half = sb("cand_half", [P, BATCH, 2 * WIDE], f32)
        node_base = sb("node_base", [P, 1], f32)
        top = sb("top", [P, BATCH, WIDE], f32)
        skip = sb("skip", [P, BATCH, SLOTS], f32)
        index = sb("index", [P, 2, BATCH, SLOTS], u32)
        valid = sb("valid", [P, 2, BATCH, SLOTS], f32)
        masked = sb("masked", [P, 2, BATCH, SLOTS], f32)
        rec = sb("rec", [P, BATCH, REC], f32)
        is_wide = sb("is_wide", [P, BATCH], bf16)
        wide_base = sb("wide_base", [P, 1], f32)
        pos = sb("pos", [P, BATCH], f32)
        one_hot = sb("one_hot", [P, BATCH, P], f32)
        unfit = sb("unfit", [P, 4, BATCH], f32)
        unfit_top = sb("unfit_top", [P, 1], f32)
        zeros = sb("zeros", [P, REC], f32)
        unfit_all = sb("unfit_all", [P, 1], f32)
        unfit_n = sb("unfit_n", [P, 1], i32)
        x_out = sb("x_out", [P, 2, BATCH, F], f32)
        e = sb("e", [P, BATCH, SLOTS], f32)
        e2 = sb("e2", [P, BATCH, SLOTS], f32)
        prob = sb("prob", [P, BATCH, SLOTS], f32)
        weight = sb("weight", [P, BATCH, SLOTS], f32)
        m4 = sb("m4", [P, BATCH], f32)
        l4 = sb("l4", [P, BATCH], f32)
        alone = sb("alone", [P, BATCH], f32)
        w_rec = sb("w_rec", [P, REC], f32)
        w_gathered = sb("w_gathered", [P, WIDE, ROW], f32)
        w_index = sb("w_index", [P, WIDE + 1], u32)
        w_valid = sb("w_valid", [P, WIDE], f32)
        w_tmp = sb("w_tmp", [P, 3, WIDE], f32)
        w_x = sb("w_x", [P, F], f32)
        w_m = sb("w_m", [P, 2], f32)
        cols = sb("cols", [P, 4], f32)

        w_t = x_out[:, 0, 0]
        diff, column = x_out[:, 1, 0].bitcast(i32), x_out[:, 1, 1].bitcast(i32)
        row_sum = one_hot
        w_flat = w_gathered[:, :, :].rearrange("p k n -> p (k n)")
        key_parts = w_flat[:, 0:2 * BIT_COLS].bitcast(i32).rearrange("p (a n) -> p a n", a=2)
        key_tmp = w_flat[:, 2 * BIT_COLS:3 * BIT_COLS]

        banks = ctx.enter_context(nc.psum_tensor("banks", [P, 8, 512], f32))

        dve_step = sem("dve_step")
        x_loaded = [sem(f"x_loaded{k}") for k in range(4)]
        w_loaded, iotas, const_made = sem("w_loaded"), sem("iotas"), sem("const_made")
        w_transposed, w_copied, wa_made, w_ready = sem("w_transposed"), sem("w_copied"), sem("wa_made"), sem("w_ready")
        var_made, std_made, normed_ready, transposed = sem("var_made"), sem("std_made"), sem("normed_ready"), sem("transposed")
        relu_ready, projected, rows_ready, summed = sem("relu_ready"), sem("projected"), sem("rows_ready"), sem("summed")
        rows_stored = [sem("rows_stored0"), sem("rows_stored1")]
        mean_summed, mean_ready = sem("mean_summed"), sem("mean_ready")
        adj_loaded = [sem(f"adj_loaded{u}") for u in range(BATCH * HALVES)]
        mask_ready, half_packed, words_read = sem("mask_ready"), sem("half_packed"), sem("words_read")
        index_ready = sem("index_ready")
        gathers_done = [sem("gathers_done0"), sem("gathers_done1")]
        x_tile = [sem("x_tile0"), sem("x_tile1")]
        out_stored = [sem("out_stored0"), sem("out_stored1")]
        logits_ready, exp_ready, out_ready = sem("logits_ready"), sem("exp_ready"), sem("out_ready")
        wide_flagged, prefix_ready, one_hot_ready, records_added = (
            sem("wide_flagged"), sem("prefix_ready"), sem("one_hot_ready"), sem("records_added"))
        records_closed, records_read = sem("records_closed"), sem("records_read")
        w_index_ready, w_gathers, w_logits, w_exp, w_out_ready, w_stored = (
            sem("w_index_ready"), sem("w_gathers"), sem("w_logits"), sem("w_exp"), sem("w_out_ready"), sem("w_stored"))
        unfit_ready, unfit_summed, verdict = sem("unfit_ready"), sem("unfit_summed"), sem("verdict")
        dn_diag, dn_bcast, dn_adj, dn_x, dn_h, dn_out = (
            sem("dn_diag"), sem("dn_bcast"), sem("dn_adj"), sem("dn_x"), sem("dn_h"), sem("dn_out"))
        dn_row, dn_step, dn_sum, pool_step = sem("dn_row"), sem("dn_step"), sem("dn_sum"), sem("pool_step")
        keys_made, a_loaded = sem("keys_made"), sem("a_loaded")
        dn_max, dn_exp, dn_blk, dn_tr, dn_pt, dn_mm, dn_o = (
            sem("dn_max"), sem("dn_exp"), sem("dn_blk"), sem("dn_tr"), sem("dn_pt"), sem("dn_mm"), sem("dn_o"))

        block = ctx.enter_context(nc.Block())

        @block.sync
        def _(sp):
            for k in range(4):
                sp.dma_start(x_all[:, k * QUARTER:(k + 1) * QUARTER, :],
                             x[k * QUARTER * P:(k + 1) * QUARTER * P, :].rearrange("(t p) f -> p t f", p=P)
                             ).then_inc(x_loaded[k], 16)

            def load_batch(i):
                for b in range(BATCH):
                    for h in range(HALVES):
                        u = b * HALVES + h
                        if i is not first:
                            sp.wait_ge(mask_ready, i * (BATCH * HALVES) + u + 1 - AHEAD)
                        sp.dma_start(adj_buf[:, u, :], adj[bass.ds((i * BATCH + b) * P, P), h * HALF:(h + 1) * HALF]
                                     ).then_inc(adj_loaded[u], 16)

            first = 0
            load_batch(first)
            with sp.Fori(1, BATCHES) as i:
                load_batch(i)

            for par in (0, 1):
                sp.wait_ge(out_stored[par], 16 * (BATCHES // 2))
            sp.wait_ge(w_stored, 16 * GROUPS)
            sp.wait_ge(verdict, 1)
            unfit_nodes = sp.value_load(unfit_n[0:1, 0:1], min_val=0, max_val=N)
            with sp.If(unfit_nodes > 0):
                sp.nop().then_inc(dn_out, 16)
                with sp.Fori(0, TILES) as t:
                    sp.wait_ge(dn_o, t + 1)
                    sp.dma_start(dense_adj, adj[bass.ts(t, P), :]).then_inc(dn_adj, 16)
                    sp.dma_start(x_row, x[bass.ts(t, P), :]).then_inc(dn_x, 16)
                    with sp.Fori(0, TILES // 4) as j:
                        sp.wait_ge(dn_mm, t * (TILES // 4) + j + 1)
                        sp.dma_start(h_blk, table[bass.ts(j, 4 * P), 0:F].rearrange("(b p) f -> p b f", p=P)).then_inc(dn_h, 16)
                    sp.wait_ge(dn_o, t + 2)
                    sp.dma_start(out[bass.ts(t, P), :], o_row).then_inc(dn_out, 16)
                sp.wait_ge(dn_out, 16 * (TILES + 1))

        @block.gpsimd
        def _(pool):
            nc.gpsimd.iota(diff, [[1, P]], base=0, channel_multiplier=-1).then_inc(iotas, 1)
            nc.gpsimd.iota(column, [[1, P]], base=1, channel_multiplier=0).then_inc(iotas, 1)
            nc.gpsimd.iota(node0[:], [[P, BATCH]], base=0, channel_multiplier=1).then_inc(iotas, 1)
            nc.gpsimd.iota(key_parts[:, 0, :], [[0, 2], [1, 256]], base=0, channel_multiplier=0).then_inc(iotas, 1)
            nc.gpsimd.iota(key_parts[:, 1, :], [[1, 2], [0, 256]], base=0, channel_multiplier=0).then_inc(iotas, 1)
            nc.gpsimd.memset(w_x[:], 0.0).then_inc(iotas, 1)
            nc.gpsimd.memset(pool_fence[:], 0.0).then_inc(pool_step, 1)
            nc.gpsimd.memset(row_sum[:], 0.0).then_inc(summed, 1)
            with pool.Fori(0, BATCHES // 2) as q:
                for par in (0, 1):
                    pool.wait_ge(rows_ready, 2 * q + par + 1)
                    pool.wait_ge(summed, 2 * q + par + 1)
                    nc.gpsimd.tensor_tensor(row_sum[:], row_sum[:], rows[par][:, :, 0:F], ALU.add).then_inc(summed, 1)

            for par in (0, 1):
                pool.wait_ge(rows_stored[par], 16 * (BATCHES // 2))
            pool.wait_ge(normed_ready, BATCHES)

            def gather_batch(i, par, first):
                if not first:
                    pool.wait_ge(out_ready, i - 1)
                pool.wait_ge(index_ready, i + 1)
                pool.wait_ge(pool_step, i + 1)
                nc.gpsimd.tensor_tensor(pool_fence[:], pool_fence[:], pool_fence[:], ALU.add).then_inc(pool_step, 1)
                for b in range(BATCH):
                    for k in range(SLOTS):
                        nc.gpsimd.indirect_dma_start(
                            g_view[par][:, b, k, :], None, table,
                            bass.IndirectOffsetOnAxis(index[:, par, b, k:k + 1], 0),
                            bounds_check=N - 1, oob_is_err=False).then_inc(gathers_done[par], 16)

            def gather_pair(q, first=False):
                for par in (0, 1):
                    gather_batch(2 * q + par, par, first)

            def wide_gather(g):
                pool.wait_ge(w_index_ready, g + 1)
                for k in range(WIDE):
                    nc.gpsimd.indirect_dma_start(
                        w_gathered[:, k, :], None, table, bass.IndirectOffsetOnAxis(w_index[:, k:k + 1], 0),
                        bounds_check=N - 1, oob_is_err=False).then_inc(w_gathers, 16)
                nc.gpsimd.indirect_dma_start(
                    w_x[:], None, x, bass.IndirectOffsetOnAxis(w_index[:, WIDE:WIDE + 1], 0),
                    bounds_check=N - 1, oob_is_err=False).then_inc(w_gathers, 16)

            def wide_store(g):
                for par in (0, 1):
                    pool.wait_ge(out_stored[par], 16 * (GROUP_BATCHES // 2) * (g + 1))
                pool.wait_ge(w_out_ready, g + 1)
                nc.gpsimd.indirect_dma_start(
                    out, bass.IndirectOffsetOnAxis(w_index[:, WIDE:WIDE + 1], 0), w_x[:], None,
                    bounds_check=N - 1, oob_is_err=False).then_inc(w_stored, 16)

            gather_pair(0, first=True)
            with pool.Fori(1, 4) as q:
                gather_pair(q)
            wide_gather(0)
            gather_pair(4)
            wide_store(0)
            with pool.Fori(5, 8) as q:
                gather_pair(q)
            wide_gather(1)
            wide_store(1)

        @block.scalar
        def _(act):
            act.dma_start(w_ext[:, 0:F], W).then_inc(w_loaded, 16)
            for k in (0, 1):
                act.dma_start(a_sb[:, k:k + 1], a[k * F:(k + 1) * F, :]).then_inc(a_loaded, 16)
            act.wait_ge(w_transposed, 1)
            nc.scalar.copy(w_t, banks[:, 6, 0:P]).then_inc(w_copied, 1)
            act.wait_ge(wa_made, 1)
            nc.scalar.copy(w_ext[:, S_COL:ROW], banks[:, 7, 0:2]).then_inc(w_ready, 1)
            def take_std(k):
                act.wait_ge(var_made, k + 1)
                mine = slice(k * QUARTER, (k + 1) * QUARTER)
                nc.scalar.activation(std[:, mine], var_e[:, mine], ACT.Sqrt).then_inc(std_made, 1)

            def relu_rows(g, par):
                act.wait_ge(transposed, g + 1)
                if not starts(g):
                    act.wait_ge(projected, g - 1)
                nc.scalar.activation(relu_t[par], banks[:, par, :].rearrange("p (b f) -> p b f", b=BATCH), ACT.Relu
                                     ).then_inc(relu_ready, 1)

            def store_rows(g, par):
                act.wait_ge(rows_ready, g + 1)
                act.dma_start(table[bass.ds(g * (BATCH * P), BATCH * P), :].rearrange("(b p) n -> p b n", p=P), rows[par]
                              ).then_inc(rows_stored[par], 16)

            take_std(0)
            for k in range(4):
                if k < 3:
                    take_std(k + 1)
                for g in range(k * (QUARTER // BATCH), (k + 1) * (QUARTER // BATCH)):
                    relu_rows(g, g % 2)
                    if g:
                        store_rows(g - 1, 1 - g % 2)
            store_rows(BATCHES - 1, 1)

            def load_x(i, par, earlier):
                act.wait_ge(out_stored[par], 16 * earlier)
                act.dma_start(x_out[:, par], x[bass.ds(i * (BATCH * P), BATCH * P), :].rearrange("(b p) f -> p b f", p=P)
                              ).then_inc(x_tile[par], 16)

            def softmax_and_store(i, par):
                act.wait_ge(logits_ready, i + 1)
                nc.scalar.activation(prob[:], e2[:], ACT.Exp).then_inc(exp_ready, 1)
                act.wait_ge(out_ready, i + 1)
                act.dma_start(out[bass.ds(i * (BATCH * P), BATCH * P), :].rearrange("(b p) f -> p b f", p=P),
                              x_out[:, par]).then_inc(out_stored[par], 16)

            def main_pair(q, first=False):
                load_x(2 * q, 0, q)
                if not first:
                    softmax_and_store(2 * q - 1, 1)
                load_x(2 * q + 1, 1, q)
                softmax_and_store(2 * q, 0)

            def wide_softmax(g):
                act.wait_ge(w_logits, g + 1)
                nc.scalar.activation(w_tmp[:, 2], w_tmp[:, 0], ACT.Exp, bias=w_m[:, 0:1], accum_out=w_m[:, 1:2]
                                     ).then_inc(w_exp, 1)

            main_pair(0, first=True)
            with act.Fori(1, 4) as q:
                main_pair(q)
            main_pair(4)
            wide_softmax(0)
            with act.Fori(5, 8) as q:
                main_pair(q)
            softmax_and_store(BATCHES - 1, 1)
            wide_softmax(1)

            act.wait_ge(verdict, 1)
            unfit_nodes = act.value_load(unfit_n[0:1, 0:1], min_val=0, max_val=N)
            with act.If(unfit_nodes > 0):
                act.nop().then_inc(dn_pt, 1)
                with act.Fori(0, TILES) as t:
                    act.wait_ge(dn_max, t + 1)
                    nc.scalar.activation(dense_e, dense_e, ACT.Exp, bias=cols[:, 0:1], accum_out=cols[:, 1:2]
                                         ).then_inc(dn_exp, 1)
                    act.wait_ge(dn_exp, t + 1)
                    with act.Fori(0, TILES // 4) as j:
                        act.wait_ge(dn_tr, t * (TILES // 4) + j + 1)
                        nc.scalar.copy(e_blk, dense_e[:, bass.ds(j * (4 * P), 4 * P)].rearrange("p (b f) -> p b f", b=4)
                                       ).then_inc(dn_blk, 1)
                        act.wait_ge(dn_tr, t * (TILES // 4) + j + 2)
                        act.wait_ge(dn_mm, t * (TILES // 4) + j + 1)
                        nc.scalar.copy(p_t, banks[:, 4, :].rearrange("p (b f) -> p b f", b=4)).then_inc(dn_pt, 1)

        @block.vector
        def _(dve):
            done = Count(dve_step)

            def settled():
                dve.wait_ge(dve_step, done.value())

            def fenced():
                settled()
                done.add(nc.vector.memset(fence[:], 0.0))

            v = nc.vector
            done.add(v.memset(ones[:], 1.0))
            done.add(v.memset(ones_b[:], 1.0))
            done.add(v.memset(zeros[:], 0.0))
            done.add(v.memset(wide_base[:], 1.0))
            done.add(v.memset(node_base[:], 0.0))
            done.add(v.memset(unfit_all[:], 0.0))
            done.add(v.memset(gathered[:, 1, N - BATCH * SLOTS * ROW:], 0.0))
            dve.wait_ge(iotas, 6)
            done.add(v.tensor_scalar(ident[:], diff, 0.0, None, ALU.is_equal))
            done.add(v.tensor_scalar(before[:], diff, 0.0, None, ALU.is_gt))
            done.add(v.tensor_copy(column_1[:], column))
            settled()
            v.memset(rec[:], 1.0).then_inc(const_made, 1)

            def statistics(k):
                first_tile = k * QUARTER
                dve.wait_ge(x_loaded[k], 16)
                for half in (0, 1):
                    settled()
                    for b in range(QUARTER // 2):
                        done.add(v.bn_stats(stats[:, b], x_all[:, first_tile + half * (QUARTER // 2) + b, :]))
                    settled()
                    for b in range(QUARTER // 2):
                        done.add(v.bn_aggr(mv_all[:, first_tile + half * (QUARTER // 2) + b, :], stats[:, b]))
                settled()
                mine = slice(first_tile, first_tile + QUARTER)
                v.tensor_scalar(var_e[:, mine], mv_all[:, mine, 1], EPS, None, ALU.add).then_inc(var_made, 1)
                dve.wait_ge(std_made, k + 1)
                done.add(v.reciprocal(rstd[:, mine], std[:, mine]))
                settled()
                done.add(v.tensor_tensor(newton[:], rstd[:, mine], rstd[:, mine], ALU.mult))
                settled()
                done.add(v.tensor_tensor(newton[:], newton[:], var_e[:, mine], ALU.mult))
                settled()
                done.add(v.tensor_scalar(newton[:], newton[:], -0.5, 1.5, ALU.mult, ALU.add))
                settled()
                done.add(v.tensor_tensor(rstd[:, mine], rstd[:, mine], newton[:], ALU.mult))
                settled()

            def normalize(g, par):
                if not starts(g):
                    dve.wait_ge(transposed, g - 1)
                for b in range(BATCH):
                    ins = v.tensor_scalar(normed[par][:, b], x_all[:, g * BATCH + b, :],
                                          mv_all[:, g * BATCH + b, 0:1], rstd[:, bass.ds(g * BATCH + b, 1)],
                                          ALU.subtract, ALU.mult)
                ins.then_inc(normed_ready, 1)

            def take_rows(g, par):
                dve.wait_ge(projected, g + 1)
                if not starts(g):
                    dve.wait_ge(summed, g)
                    dve.wait_ge(rows_stored[par], 16 * (g // 2))
                pair = banks[:, 2 + 2 * par:4 + 2 * par, 0:2 * ROW]
                done.add(v.tensor_copy(sd_all[:, bass.ds(g * BATCH, BATCH), :].rearrange("p (u w) c -> p u w c", u=2),
                                       pair.rearrange("p u (w n) -> p u w n", w=2)[:, :, :, S_COL:ROW]))
                v.tensor_copy(rows[par].rearrange("p (u w) n -> p u (w n)", u=2), pair).then_inc(rows_ready, 1)

            statistics(0)
            for g in (0, 1):
                normalize(g, g)
            for k in range(4):
                if k < 3:
                    statistics(k + 1)
                for g in range(k * (QUARTER // BATCH), (k + 1) * (QUARTER // BATCH)):
                    if g + 2 < BATCHES:
                        normalize(g + 2, g % 2)
                    take_rows(g, g % 2)

            for c in range(HALF_BITS):
                done.add(v.tensor_scalar(bit_ident[:, c], ident[:], float(1 << c), None, ALU.mult))
            done.add(v.tensor_scalar(key_tmp, key_parts[:, 0], ident[:, 0:1], 1.0 / BIT_COLS, ALU.mult, ALU.mult))
            settled()
            done.add(v.tensor_scalar(rest[:], key_parts[:, 1], ident[:, 1:2], 256.0 / BIT_COLS, ALU.mult, ALU.mult))
            settled()
            done.add(v.tensor_tensor(key_tmp, key_tmp, rest[:], ALU.add))
            settled()
            done.add(v.tensor_scalar(fence[:], ident[:, 2:3], -float(1 << (BITS - 1)), None, ALU.mult))
            settled()
            v.tensor_scalar(key_rows[:], key_tmp, fence[:, 0:1], None, ALU.add).then_inc(keys_made, 1)
            dve.wait_ge(keys_made, 1)
            done.add(v.memset(w_gathered[:], 0.0))
            for par in (0, 1):
                dve.wait_ge(rows_stored[par], 16 * (BATCHES // 2))
            dve.wait_ge(summed, BATCHES + 1)
            dve.wait_ge(projected, BATCHES)
            dve.wait_ge(mean_summed, 1)
            done.add(v.tensor_scalar(mean_h[:], banks[:, 6, 0:F], 1.0 / N, None, ALU.mult))

            def compare(i, b, h, words_of=None):
                unit = i * (BATCH * HALVES) + b * HALVES + h
                dve.wait_ge(adj_loaded[b * HALVES + h], 16 * i + 16)
                if not (starts_int(i) and b == 0):
                    dve.wait_ge(half_packed, unit - 1)
                if words_of is not None:
                    dve.wait_ge(half_packed, 2 * (i * BATCH + words_of) + 2)
                    dve.wait_ge(words_read, i * BATCH + words_of)
                settled()
                v.tensor_scalar(mask_buf[:, h], adj_buf[:, b * HALVES + h], 0.0, float(1 << h * HALF_BITS),
                                ALU.is_gt, ALU.mult).then_inc(mask_ready, 1)

            def first_words(b):
                done.add(v.max(words[:, b, 0:8], banks[:, b % 2]))

            def remove_words(b):
                v.match_replace(rest[:], words[:, b, 0:8], banks[:, b % 2], -float(1 << BITS)).then_inc(words_read, 1)

            def second_words(b):
                done.add(v.max(words[:, b, 8:16], rest[:]))

            def decode(i, par):
                done.add(v.tensor_scalar(wi[0][:], words[:], float(BIT_COLS), None, ALU.mult))
                settled()
                done.add(v.tensor_scalar(wi[1][:], wi[0][:], BIT_COLS - 1, None, ALU.bitwise_and))
                done.add(v.tensor_scalar(wi[2][:], wi[0][:], 9, None, ALU.arith_shift_right))
                settled()
                done.add(v.tensor_scalar(wf[0][:], wi[2][:], float(1 << (BITS - 1)), None, ALU.add))
                settled()
                done.add(v.tensor_scalar(wi[0][:], wf[0][:].bitcast(i32), 23, None, ALU.logical_shift_right))
                done.add(v.tensor_scalar(top_bit[:], wf[0][:].bitcast(i32), 0x7F800000, None, ALU.bitwise_and))
                settled()
                done.add(v.scalar_tensor_tensor(cand[:, :, 0:WIDE], wi[0][:], float(BIT_COLS), wi[1][:], ALU.mult, ALU.add))
                done.add(v.tensor_tensor(wf[1][:], wf[0][:], top_bit[:].bitcast(f32), ALU.subtract))
                settled()
                done.add(v.tensor_scalar(wi[2][:], wf[1][:].bitcast(i32), 23, None, ALU.logical_shift_right))
                done.add(v.tensor_scalar(top_bit[:], wf[1][:].bitcast(i32), 0x7F800000, None, ALU.bitwise_and))
                settled()
                done.add(v.scalar_tensor_tensor(cand[:, :, WIDE:], wi[2][:], float(BIT_COLS), wi[1][:], ALU.mult, ALU.add))
                done.add(v.tensor_tensor(wf[2][:], wf[1][:], top_bit[:].bitcast(f32), ALU.subtract))
                settled()
                done.add(v.tensor_reduce(unfit[:, 0], wf[2][:], AX.X, ALU.max))
                done.add(v.tensor_copy(unfit[:, 1], wf[0][:, :, WIDE - 1]))
                settled()
                done.add(v.tensor_scalar(cand_half[:], cand[:], float(EXP_BIAS), 0.5, ALU.is_ge, ALU.subtract))
                settled()
                done.add(v.tensor_reduce(unfit[:, 2], cand_half[:], AX.X, ALU.add))
                for b in range(BATCH):
                    done.add(v.max(top[:, b, 0:8], cand[:, b]))
                fenced()
                for b in range(BATCH):
                    done.add(v.match_replace(cand[:, b], top[:, b, 0:8], cand[:, b], 0.0))
                fenced()
                for b in range(BATCH):
                    done.add(v.max(top[:, b, 8:16], cand[:, b]))
                settled()
                done.add(v.tensor_scalar(skip[:], top[:, :, 0:SLOTS], float(EXP_BIAS), SKIP, ALU.is_lt, ALU.mult))
                done.add(v.tensor_scalar(valid[:, par], top[:, :, 0:SLOTS], float(EXP_BIAS), None, ALU.is_ge))
                settled()
                v.scalar_tensor_tensor(index[:, par], top[:, :, 0:SLOTS], -float(EXP_BIAS), skip[:],
                                       ALU.add, ALU.add).then_inc(index_ready, 1)
                done.add(v.tensor_scalar(masked[:, par], valid[:, par], 1.0, MASKED, ALU.subtract, ALU.mult))
                if not starts_int(i):
                    dve.wait_ge(records_added, i)
                done.add(v.tensor_copy(rec[:, :, 0:WIDE], top[:]))
                done.add(v.tensor_copy(rec[:, :, REC_S], sd_all[:, bass.ds(i * BATCH, BATCH), 0]))
                done.add(v.tensor_scalar(rec[:, :, REC_NODE], node0[:], node_base[:, 0:1], None, ALU.add))
                settled()
                done.add(v.tensor_scalar(node_base[:], node_base[:], float(BATCH * P), None, ALU.add))
                v.tensor_scalar(is_wide[:], top[:, :, SLOTS], float(EXP_BIAS), None, ALU.is_ge).then_inc(wide_flagged, 1)

            def place_wide(i):
                dve.wait_ge(prefix_ready, i + 1)
                done.add(v.scalar_tensor_tensor(pos[:], banks[:, 2, 0:BATCH], wide_base[:, 0:1], is_wide[:], ALU.add, ALU.mult))
                settled()
                done.add(v.tensor_tensor(wide_base[:], wide_base[:], banks[:, 2, BATCH:BATCH + 1], ALU.add))
                done.add(v.tensor_scalar(unfit[:, 3], pos[:], float(P), None, ALU.subtract))
                for b in range(BATCH):
                    ins = v.tensor_scalar(one_hot[:, b], column_1[:], pos[:, b:b + 1], None, ALU.is_equal)
                ins.then_inc(one_hot_ready, 1)
                settled()
                done.add(v.tensor_reduce(unfit_top[:], unfit[:], AX.XY, ALU.max))
                settled()
                done.add(v.tensor_tensor(unfit_all[:], unfit_all[:], unfit_top[:], ALU.max))

            def logits(i, par, gathered_times):
                d = g_view[par][:, :, :, D_COL]
                s = sd_all[:, bass.ds(i * BATCH, BATCH), 0:1].to_broadcast([P, BATCH, SLOTS])
                dve.wait_ge(gathers_done[par], 16 * BATCH * SLOTS * gathered_times)
                settled()
                done.add(v.tensor_tensor(e[:], d, s, ALU.add))
                settled()
                done.add(v.scalar_tensor_tensor(e2[:], e[:], ALPHA, e[:], ALU.mult, ALU.max))
                settled()
                done.add(v.tensor_tensor(e[:], e2[:], valid[:, par], ALU.mult))
                settled()
                done.add(v.tensor_tensor(e[:], e[:], masked[:, par], ALU.add))
                settled()
                done.add(v.tensor_reduce(m4[:], e[:], AX.X, ALU.max))
                settled()
                v.tensor_tensor(e2[:], e[:], m4[:].unsqueeze(2).to_broadcast([P, BATCH, SLOTS]), ALU.subtract
                                ).then_inc(logits_ready, 1)

            def weighted_sum(i, par, gathered_times):
                dve.wait_ge(exp_ready, i + 1)
                done.add(v.tensor_tensor(weight[:], prob[:], valid[:, par], ALU.mult))
                settled()
                done.add(v.tensor_reduce(l4[:], weight[:], AX.X, ALU.add))
                settled()
                done.add(v.tensor_scalar(alone[:], l4[:], 0.5, None, ALU.is_lt))
                done.add(v.tensor_scalar(m4[:], l4[:], 0.5, None, ALU.max))
                settled()
                done.add(v.reciprocal(l4[:], m4[:]))
                settled()
                done.add(v.tensor_tensor(weight[:], weight[:], l4[:].unsqueeze(2).to_broadcast([P, BATCH, SLOTS]), ALU.mult))
                dve.wait_ge(x_tile[par], 16 * gathered_times)
                for b in range(BATCH):
                    done.add(v.scalar_tensor_tensor(x_out[:, par, b], mean_h[:], alone[:, b:b + 1], x_out[:, par, b],
                                                    ALU.mult, ALU.add))
                for k in range(SLOTS):
                    settled()
                    for b in range(BATCH):
                        ins = v.scalar_tensor_tensor(x_out[:, par, b], g_view[par][:, b, k, 0:F], weight[:, b, k:k + 1],
                                                     x_out[:, par, b], ALU.mult, ALU.add)
                        if k < SLOTS - 1 or b < BATCH - 1:
                            done.add(ins)
                ins.then_inc(out_ready, 1)

            def step(i, par, q, first=False):
                compare(i, 0, 0)
                compare(i, 0, 1)
                compare(i, 1, 0)
                compare(i, 1, 1, words_of=0)
                first_words(0)
                compare(i, 2, 0)
                remove_words(0)
                compare(i, 2, 1, words_of=1)
                second_words(0)
                first_words(1)
                compare(i, 3, 0)
                remove_words(1)
                compare(i, 3, 1, words_of=2)
                second_words(1)
                first_words(2)
                fenced()
                remove_words(2)
                dve.wait_ge(words_read, i * BATCH + 3)
                dve.wait_ge(half_packed, 2 * (i * BATCH + 3) + 2)
                fenced()
                second_words(2)
                first_words(3)
                fenced()
                remove_words(3)
                dve.wait_ge(words_read, i * BATCH + 4)
                fenced()
                second_words(3)
                settled()
                decode(i, par)
                if not first:
                    logits(i - 1, 1 - par, q + par)
                place_wide(i)
                if not first:
                    weighted_sum(i - 1, 1 - par, q + par)

            def main_pair(q, first=False):
                step(2 * q, 0, q, first)
                step(2 * q + 1, 1, q)

            def wide_index(g):
                dve.wait_ge(records_closed, g + 1)
                if g:
                    dve.wait_ge(w_stored, 16 * g)
                settled()
                v.tensor_copy(w_rec[:], banks[:, 3, 0:REC]).then_inc(records_read, 1)
                dve.wait_ge(records_read, g + 1)
                done.add(v.memset(wide_base[:], 1.0))
                done.add(v.tensor_scalar(w_tmp[:, 0], w_rec[:, 0:WIDE], float(EXP_BIAS), SKIP, ALU.is_lt, ALU.mult))
                done.add(v.tensor_scalar(w_valid[:], w_rec[:, 0:WIDE], float(EXP_BIAS), None, ALU.is_ge))
                done.add(v.tensor_scalar(w_m[:, 0:1], w_rec[:, REC_ONE:REC_ONE + 1], -SKIP, SKIP, ALU.mult, ALU.add))
                settled()
                done.add(v.scalar_tensor_tensor(w_index[:, 0:WIDE], w_rec[:, 0:WIDE], -float(EXP_BIAS), w_tmp[:, 0],
                                                ALU.add, ALU.add))
                settled()
                v.tensor_tensor(w_index[:, WIDE:WIDE + 1], w_rec[:, REC_NODE:REC_NODE + 1], w_m[:, 0:1], ALU.add
                                ).then_inc(w_index_ready, 1)

            def wide_sum(g):
                dve.wait_ge(w_gathers, 16 * (WIDE + 1) * (g + 1))
                settled()
                done.add(v.tensor_scalar(w_tmp[:, 0], w_gathered[:, :, D_COL], w_rec[:, REC_S:REC_S + 1], None, ALU.add))
                settled()
                done.add(v.scalar_tensor_tensor(w_tmp[:, 1], w_tmp[:, 0], ALPHA, w_tmp[:, 0], ALU.mult, ALU.max))
                settled()
                done.add(v.tensor_tensor(w_tmp[:, 0], w_tmp[:, 1], w_valid[:], ALU.mult))
                settled()
                done.add(v.tensor_scalar(w_tmp[:, 1], w_valid[:], 1.0, MASKED, ALU.subtract, ALU.mult))
                settled()
                done.add(v.tensor_tensor(w_tmp[:, 0], w_tmp[:, 0], w_tmp[:, 1], ALU.add))
                settled()
                v.tensor_reduce(w_m[:, 0:1], w_tmp[:, 0], AX.X, ALU.max, negate=True).then_inc(w_logits, 1)
                dve.wait_ge(w_exp, g + 1)
                done.add(v.reciprocal(w_m[:, 1:2], w_m[:, 1:2]))
                settled()
                done.add(v.tensor_scalar(w_tmp[:, 2], w_tmp[:, 2], w_m[:, 1:2], None, ALU.mult))
                for k in range(WIDE):
                    settled()
                    ins = v.scalar_tensor_tensor(w_x[:], w_gathered[:, k, 0:F], w_tmp[:, 2, k:k + 1], w_x[:], ALU.mult, ALU.add)
                    if k < WIDE - 1:
                        done.add(ins)
                ins.then_inc(w_out_ready, 1)


            def looped(lo, hi):
                with dve.Fori(lo, hi) as q:
                    done.enter(q - lo, 2 * DVE_STEPS)
                    main_pair(q)
                    done.leave(hi - lo)

            main_pair(0, first=True)
            looped(1, 4)
            wide_index(0)
            main_pair(4)
            wide_sum(0)
            looped(5, 8)
            wide_index(1)
            logits(BATCHES - 1, 1, BATCHES // 2)
            weighted_sum(BATCHES - 1, 1, BATCHES // 2)
            wide_sum(1)

            settled()
            v.tensor_scalar(unfit_top[:], unfit_all[:], 0.0, None, ALU.is_gt).then_inc(unfit_ready, 1)
            dve.wait_ge(unfit_summed, 1)
            v.tensor_copy(unfit_n[:], banks[:, 4, 0:1]).then_inc(verdict, 1)
            dve.wait_ge(verdict, 1)
            unfit_nodes = dve.value_load(unfit_n[0:1, 0:1], min_val=0, max_val=N)
            with dve.If(unfit_nodes > 0):
                dve.nop().then_inc(dn_row, 1)
                dve.nop().then_inc(dn_o, 1)
                dve.nop().then_inc(dn_step, 1)
                with dve.Fori(0, TILES) as j:
                    dve.wait_ge(dn_bcast, j + 1)
                    v.tensor_scalar(d_diag, ident[:], sd_all[:, j, 1:2], None, ALU.mult).then_inc(dn_diag, 1)
                    dve.wait_ge(dn_bcast, j + 2)
                    v.tensor_copy(dense_d[:, bass.ds(j * P, P)], banks[:, 4, 0:P]).then_inc(dn_row, 1)
                dve.wait_ge(dn_row, TILES + 1)
                v.memset(d_diag, 0.0).then_inc(dn_row, 1)
                with dve.Fori(0, TILES) as t:
                    dense = Count(dn_step, credit=1)
                    dense.enter(t, 8)

                    def dense_settled():
                        dve.wait_ge(dn_step, dense.value())

                    dve.wait_ge(dn_adj, 16 * t + 16)
                    dve.wait_ge(dn_tr, t * (TILES // 4) + 1)
                    dense.add(v.tensor_scalar(dense_e, dense_d, sd_all[:, t, 0:1], None, ALU.add))
                    dense.add(v.tensor_scalar(dense_m, dense_adj, 0.0, None, ALU.is_gt))
                    dense_settled()
                    dense.add(v.scalar_tensor_tensor(dense_e, dense_e, ALPHA, dense_e, ALU.mult, ALU.max))
                    dense_settled()
                    dense.add(v.tensor_tensor(dense_e, dense_e, dense_m, ALU.mult))
                    dense_settled()
                    dense.add(v.tensor_scalar(dense_m, dense_m, 1.0, MASKED, ALU.subtract, ALU.mult))
                    dense_settled()
                    dense.add(v.tensor_tensor(dense_e, dense_e, dense_m, ALU.add))
                    dense_settled()
                    v.tensor_reduce(cols[:, 0:1], dense_e, AX.X, ALU.max, negate=True).then_inc(dn_max, 1)
                    dve.wait_ge(dn_exp, t + 1)
                    dense.add(v.reciprocal(cols[:, 2:3], cols[:, 1:2]))
                    dense_settled()
                    dve.wait_ge(dn_sum, t + 1)
                    dve.wait_ge(dn_x, 16 * t + 16)
                    dve.wait_ge(dn_out, 16 * t + 16)
                    v.scalar_tensor_tensor(o_row, banks[:, 5, 0:F], cols[:, 2:3], x_row, ALU.mult, ALU.add).then_inc(dn_o, 1)
                    dense.add(v.memset(fence[:], 0.0))

        @block.tensor
        def _(pe):
            mm = nc.tensor.matmul
            pe.wait_ge(const_made, 1)
            pe.wait_ge(w_loaded, 16)
            nc.tensor.transpose(banks[:, 6, 0:P], w_ext[:, 0:F], ident[:]).then_inc(w_transposed, 1)
            pe.wait_ge(w_copied, 1)
            pe.wait_ge(a_loaded, 32)
            mm(banks[:, 7, 0:2], w_t, a_sb[:], start=True, stop=True).then_inc(wa_made, 1)
            pe.wait_ge(w_ready, 1)

            def transpose_rows(g, par):
                pe.wait_ge(normed_ready, g + 1)
                if not starts(g):
                    pe.wait_ge(relu_ready, g - 1)
                for b in range(BATCH):
                    ins = nc.tensor.transpose(banks[:, par, b * P:(b + 1) * P], normed[par][:, b], ident[:])
                ins.then_inc(transposed, 1)

            def project(g, par):
                pe.wait_ge(relu_ready, g + 1)
                if not starts(g):
                    pe.wait_ge(rows_ready, g - 1)
                for b in range(BATCH):
                    at = b % 2 * ROW
                    ins = mm(banks[:, 2 + 2 * par + b // 2, at:at + ROW], relu_t[par][:, b], w_ext[:], start=True, stop=True)
                ins.then_inc(projected, 1)

            def project_pair(q, last=False):
                transpose_rows(2 * q + 1, 1)
                project(2 * q, 0)
                if not last:
                    transpose_rows(2 * q + 2, 0)
                project(2 * q + 1, 1)

            transpose_rows(0, 0)
            project_pair(0)
            with pe.Fori(1, BATCHES // 2 - 1) as q:
                project_pair(q)
            project_pair(BATCHES // 2 - 1, last=True)
            pe.wait_ge(summed, BATCHES + 1)
            for b in range(BATCH):
                ins = mm(banks[:, 6, 0:F], ones[:], row_sum[:, b], start=(b == 0), stop=(b == BATCH - 1))
            ins.then_inc(mean_summed, 1)
            pe.wait_ge(keys_made, 1)

            def pack(i, b, h):
                pe.wait_ge(mask_ready, i * (BATCH * HALVES) + b * HALVES + h + 1)
                if h == 0:
                    if not (starts_int(i) and b < 2):
                        pe.wait_ge(words_read, i * BATCH + b - 1)
                    mm(banks[:, b % 2], ones_b[0:3, :], key_rows[0:3, :], start=True, stop=False)
                for c in range(HALF_BITS):
                    ins = mm(banks[:, b % 2], bit_ident[:, c], mask_buf[:, h, c * BIT_COLS:(c + 1) * BIT_COLS],
                             start=False, stop=(h == 1 and c == HALF_BITS - 1))
                ins.then_inc(half_packed, 1)

            def count_wide(i):
                pe.wait_ge(wide_flagged, i + 1)
                if not starts_int(i):
                    pe.wait_ge(one_hot_ready, i)
                for b in range(BATCH):
                    mm(banks[:, 2, b:b + 1], before[:], is_wide[:, b:b + 1], start=True, stop=(b == 0))
                    for c in range(b):
                        mm(banks[:, 2, b:b + 1], ones_b[:], is_wide[:, c:c + 1], start=False, stop=(c == b - 1))
                for b in range(BATCH):
                    ins = mm(banks[:, 2, BATCH:BATCH + 1], ones_b[:], is_wide[:, b:b + 1], start=(b == 0), stop=(b == BATCH - 1))
                ins.then_inc(prefix_ready, 1)

            def add_records(i):
                pe.wait_ge(one_hot_ready, i + 1)
                for b in range(BATCH):
                    ins = mm(banks[:, 3, 0:REC], one_hot[:, b], rec[:, b], start=False, stop=False)
                ins.then_inc(records_added, 1)

            def main_pair(q, first=False):
                for i in (2 * q, 2 * q + 1):
                    for b in range(BATCH):
                        for h in range(HALVES):
                            pack(i, b, h)
                    count_wide(i)
                    add_records(i)

            def open_records():
                mm(banks[:, 3, 0:REC], ones[:], zeros[:, 0:REC], start=True, stop=False)

            def close_records():
                mm(banks[:, 3, 0:REC], ones[:], zeros[:, 0:REC], start=False, stop=True).then_inc(records_closed, 1)

            open_records()
            main_pair(0)
            with pe.Fori(1, 4) as q:
                main_pair(q)
            close_records()
            pe.wait_ge(records_read, 1)
            open_records()
            main_pair(4)
            with pe.Fori(5, 8) as q:
                main_pair(q)
            close_records()
            pe.wait_ge(unfit_ready, 1)
            mm(banks[:, 4, 0:1], ones[:], unfit_top[:], start=True, stop=True).then_inc(unfit_summed, 1)

            pe.wait_ge(verdict, 1)
            unfit_nodes = pe.value_load(unfit_n[0:1, 0:1], min_val=0, max_val=N)
            with pe.If(unfit_nodes > 0):
                pe.nop().then_inc(dn_bcast, 1)
                pe.nop().then_inc(dn_tr, 1)
                pe.nop().then_inc(dn_mm, 1)
                with pe.Fori(0, TILES) as j:
                    pe.wait_ge(dn_diag, j + 1)
                    pe.wait_ge(dn_row, j + 1)
                    mm(banks[:, 4, 0:P], ones[:], d_diag, start=True, stop=True).then_inc(dn_bcast, 1)
                pe.wait_ge(dn_row, TILES + 2)
                with pe.Fori(0, TILES) as t:
                    pe.wait_ge(dn_o, t + 1)
                    mm(banks[:, 5, 0:F], ones[:], d_diag, start=True, stop=False)
                    with pe.Fori(0, TILES // 4) as j:
                        at = t * (TILES // 4) + j
                        pe.wait_ge(dn_blk, at + 1)
                        pe.wait_ge(dn_pt, at + 1)
                        for b in range(4):
                            ins = nc.tensor.transpose(banks[:, 4, b * P:(b + 1) * P], e_blk[:, b], ident[:])
                        ins.then_inc(dn_tr, 1)
                        pe.wait_ge(dn_pt, at + 2)
                        pe.wait_ge(dn_h, 16 * at + 16)
                        for b in range(4):
                            ins = mm(banks[:, 5, 0:F], p_t[:, b], h_blk[:, b], start=False, stop=False)
                        ins.then_inc(dn_mm, 1)
                    mm(banks[:, 5, 0:F], ones[:], d_diag, start=False, stop=True).then_inc(dn_sum, 1)


def starts(g):
    return isinstance(g, int) and g < 2


def starts_int(i):
    return isinstance(i, int) and i == 0


def kernel(**inputs):
    import numpy as np
    import concourse.bacc as bacc
    from concourse.bass_utils import run_bass_kernel_spmd

    nc = bacc.Bacc("TRN2", target_bir_lowering=False, num_devices=1)
    arrays, args = {}, []
    for name in ("x", "adj", "L0_gnn_W", "L0_gnn_a"):
        arrays[f"in_{name}"] = np.ascontiguousarray(inputs[name])
        args.append(nc.dram_tensor(f"in_{name}", arrays[f"in_{name}"].shape,
                                   mybir.dt.from_np(arrays[f"in_{name}"].dtype), kind="ExternalInput").ap())
    args.append(nc.dram_tensor("out", (N, F), mybir.dt.float32, kind="ExternalOutput").ap())
    gat_kernel(nc, *args)
    return run_bass_kernel_spmd(nc, [arrays], core_ids=[0]).results[0]["out"]
```

```python
import concourse.bass as bass
from concourse import mybir
from contextlib import ExitStack

P = 128
N = 8192
F = 128
TILES = N // P
QUARTER = TILES // 4
STAT_GROUPS = [(0, 8), (8, 16), (16, 32), (32, 48), (48, 64)]
FOUR = 4
FOURS = TILES // FOUR
BATCH = 2
BATCHES = TILES // BATCH
BUFS = 4
LAG = 2
ROUNDS = BATCHES // BUFS
GROUPS = 2
GROUP_ROUNDS = ROUNDS // GROUPS
GROUP_BATCHES = BATCHES // GROUPS
BIT_COLS = 512
BITS = N // BIT_COLS
HALVES = 2
UNITS = BATCH * HALVES
HALF = N // HALVES
HALF_BITS = BITS // HALVES
STORE_LAG = 6
SLOTS = 8
WIDE = 16
ROW = F + 2
S_COL, D_COL = F, F + 1
REC = WIDE + 4
REC_S, REC_NODE, REC_ONE = WIDE, WIDE + 1, WIDE + 2
EPS = 1e-5
ALPHA = 0.2
MASKED = 9e15
EXP_BIAS = 127 * BIT_COLS
DVE_STEPS = 73
MAGIC = 0x5F3759DF
NEWTON_STEPS = 3
SKIP = 100000.0


class Count:

    def __init__(self, sem, credit=0):
        self.sem, self.base, self.n, self.total = sem, credit, 0, credit

    def add(self, ins):
        ins.then_inc(self.sem, 1)
        self.n += 1
        return self.value()

    def value(self):
        return self.base + self.n

    def enter(self, i, per):
        self.total += self.n
        self.base, self.n, self.per = i * per + self.total, 0, per

    def leave(self, times):
        assert self.n == self.per, f"{self.n} signals in the loop's body, not {self.per}"
        self.total += times * self.per
        self.base, self.n = self.total, 0


def gat_kernel(nc, x, adj, W, a, out):
    f32, bf16 = mybir.dt.float32, mybir.dt.bfloat16
    i32, u32 = mybir.dt.int32, mybir.dt.uint32
    ALU, ACT, AX = mybir.AluOpType, mybir.ActivationFunctionType, mybir.AxisListType

    table = nc.dram_tensor("table", (N, ROW), f32).ap()

    ctx = ExitStack()
    with ctx:
        def sb(name, shape, dt):
            return ctx.enter_context(nc.sbuf_tensor(name, shape, dt))

        def sem(name):
            return ctx.enter_context(nc.semaphore(name))

        adj_buf = sb("adj_buf", [P, UNITS, HALF], i32)
        mask_buf = sb("mask_buf", [P, UNITS, HALF], bf16)
        gathered = sb("gathered", [P, BUFS, BATCH * SLOTS * ROW], f32)
        g_view = [gathered[:, buf, :].rearrange("p (b k n) -> p b k n", b=BATCH, k=SLOTS) for buf in range(BUFS)]
        rows_all = gathered[:, :, :].rearrange("p a (t n) -> p (a t) n", n=ROW)
        x_all = sb("x_all", [P, TILES, F], f32)
        work = sb("work", [P, 4, FOUR, F], f32)
        normed, relu_t = [work[:, 0], work[:, 1]], [work[:, 2], work[:, 3]]
        e_blk, p_t = normed[0], relu_t[0]
        h_blk = x_all[:, 0:FOUR, :]
        x_row, o_row, d_diag = normed[1][:, 0, :], normed[1][:, 1, :], normed[1][:, 2, :]
        dense_adj = adj_buf[:, 0:2, :].rearrange("p u n -> p (u n)")
        dense_d = adj_buf[:, 2:4, :].rearrange("p u n -> p (u n)").bitcast(f32)
        dense_e = mask_buf[:, :, :].rearrange("p u n -> p (u n)").bitcast(f32)
        dense_m = gathered[:, :, :].rearrange("p a n -> p (a n)")[:, 0:N]

        w_ext = sb("w_ext", [P, ROW], f32)
        a_sb = sb("a_sb", [P, 2], f32)
        column_1 = sb("column_1", [P, P], f32)
        node0 = sb("node0", [P, BATCH], i32)
        ident = sb("ident", [P, P], f32)
        ones = sb("ones", [P, P], f32)
        ones_b = sb("ones_b", [P, P], bf16)
        before = sb("before", [P, P], bf16)
        bit_ident = sb("bit_ident", [P, BITS, P], bf16)
        minus_half = sb("minus_half", [P, 1], f32)
        key_rows = sb("key_rows", [P, BIT_COLS], bf16)
        stats = sb("stats", [P, QUARTER, 6], f32)
        mv_all = sb("mv_all", [P, TILES, 2], f32)
        rstd = sb("rstd", [P, TILES], f32)
        nbias = sb("nbias", [P, TILES], f32)
        newton = sb("newton", [P, 2, QUARTER], f32)
        r_sums = sb("r_sums", [P, FOURS], f32)
        r_sum = sb("r_sum", [P, 1], f32)
        r_sum_cols = sb("r_sum_cols", [P, P], f32)
        var_e = sb("var_e", [P, TILES], f32)
        mean_h = sb("mean_h", [P, F], f32)
        sd_all = sb("sd_all", [P, TILES, 2], f32)
        fence = sb("fence", [P, 1], f32)
        pool_fence = sb("pool_fence", [P, 1], f32)
        rest = sb("rest", [P, BIT_COLS], f32)
        words = sb("words", [P, BATCH, WIDE], f32)
        wi = [sb(f"wi{k}", [P, BATCH, WIDE], i32) for k in range(3)]
        wf = [sb(f"wf{k}", [P, BATCH, WIDE], f32) for k in range(3)]
        top_bit = sb("top_bit", [P, BATCH, WIDE], i32)
        cand = sb("cand", [P, BATCH, 2 * WIDE], f32)
        cand_half = sb("cand_half", [P, BATCH, 2 * WIDE], f32)
        node_base = sb("node_base", [P, 1], f32)
        top = sb("top", [P, BATCH, WIDE], f32)
        skip = sb("skip", [P, BATCH, SLOTS], f32)
        index = sb("index", [P, BUFS, BATCH, SLOTS], u32)
        valid = sb("valid", [P, BUFS, BATCH, SLOTS], f32)
        masked = sb("masked", [P, BUFS, BATCH, SLOTS], f32)
        rec = sb("rec", [P, BATCH, REC], f32)
        is_wide = sb("is_wide", [P, BATCH], bf16)
        wide_base = sb("wide_base", [P, 1], f32)
        pos = sb("pos", [P, BATCH], f32)
        one_hot = sb("one_hot", [P, BATCH, P], f32)
        unfit = sb("unfit", [P, 4, BATCH], f32)
        unfit_top = sb("unfit_top", [P, 1], f32)
        zeros = sb("zeros", [P, REC], f32)
        unfit_all = sb("unfit_all", [P, 1], f32)
        unfit_n = sb("unfit_n", [P, 1], i32)
        e = sb("e", [P, BATCH, SLOTS], f32)
        e2 = sb("e2", [P, BATCH, SLOTS], f32)
        prob = sb("prob", [P, BATCH, SLOTS], f32)
        weight = sb("weight", [P, BATCH, SLOTS], f32)
        m4 = sb("m4", [P, BATCH], f32)
        l4 = sb("l4", [P, BATCH], f32)
        alone = sb("alone", [P, BATCH], f32)
        w_rec = sb("w_rec", [P, REC], f32)
        w_gathered = sb("w_gathered", [P, WIDE, ROW], f32)
        w_index = sb("w_index", [P, WIDE + 1], u32)
        w_valid = sb("w_valid", [P, WIDE], f32)
        w_tmp = sb("w_tmp", [P, 3, WIDE], f32)
        w_x = sb("w_x", [P, F], f32)
        w_m = sb("w_m", [P, 2], f32)
        cols = sb("cols", [P, 4], f32)

        w_flat = w_gathered[:, :, :].rearrange("p k n -> p (k n)")
        key_parts = w_flat[:, 0:2 * BIT_COLS].bitcast(i32).rearrange("p (a n) -> p a n", a=2)
        key_tmp = w_flat[:, 2 * BIT_COLS:3 * BIT_COLS]
        diff, column, w_t = [w_flat[:, 3 * BIT_COLS + k * P:3 * BIT_COLS + (k + 1) * P] for k in range(3)]
        diff, column = diff.bitcast(i32), column.bitcast(i32)

        banks = ctx.enter_context(nc.psum_tensor("banks", [P, 8, 512], f32))

        dve_step = sem("dve_step")
        x_loaded = [sem(f"x_loaded{k}") for k in range(len(STAT_GROUPS))]
        w_loaded, iotas, const_made = sem("w_loaded"), sem("iotas"), sem("const_made")
        w_transposed, w_copied, wa_made, w_ready = sem("w_transposed"), sem("w_copied"), sem("wa_made"), sem("w_ready")
        rstd_ready, normed_act, normed_pool, transposed = (
            sem("rstd_ready"), sem("normed_act"), sem("normed_pool"), sem("transposed"))
        relu_ready, projected, rows_ready, sd_ready = sem("relu_ready"), sem("projected"), sem("rows_ready"), sem("sd_ready")
        rows_stored = [sem(f"rows_stored{k}") for k in range(4)]
        r_summed, mean_ready = sem("r_summed"), sem("mean_ready")
        adj_loaded = [sem(f"adj_loaded{u}") for u in range(UNITS)]
        mask_ready, half_packed, words_read = sem("mask_ready"), sem("half_packed"), sem("words_read")
        index_ready = sem("index_ready")
        gathers_done = [sem(f"gathers_done{k}") for k in range(BUFS)]
        out_stored = [sem(f"out_stored{g}") for g in range(GROUPS)]
        logits_ready, exp_ready, out_ready = sem("logits_ready"), sem("exp_ready"), sem("out_ready")
        wide_flagged, prefix_ready, one_hot_ready, records_added = (
            sem("wide_flagged"), sem("prefix_ready"), sem("one_hot_ready"), sem("records_added"))
        records_closed, records_read = sem("records_closed"), sem("records_read")
        w_index_ready, w_gathers, w_logits, w_exp, w_out_ready, w_stored = (
            sem("w_index_ready"), sem("w_gathers"), sem("w_logits"), sem("w_exp"), sem("w_out_ready"), sem("w_stored"))
        unfit_ready, unfit_summed, verdict = sem("unfit_ready"), sem("unfit_summed"), sem("verdict")
        dn_diag, dn_bcast, dn_adj, dn_x, dn_h, dn_out = (
            sem("dn_diag"), sem("dn_bcast"), sem("dn_adj"), sem("dn_x"), sem("dn_h"), sem("dn_out"))
        dn_row, dn_step, dn_sum, pool_step = sem("dn_row"), sem("dn_step"), sem("dn_sum"), sem("pool_step")
        keys_made, a_loaded = sem("keys_made"), sem("a_loaded")
        dn_max, dn_exp, dn_blk, dn_tr, dn_pt, dn_mm, dn_o = (
            sem("dn_max"), sem("dn_exp"), sem("dn_blk"), sem("dn_tr"), sem("dn_pt"), sem("dn_mm"), sem("dn_o"))

        block = ctx.enter_context(nc.Block())

        @block.sync
        def _(sp):
            for k, (lo, hi) in enumerate(STAT_GROUPS):
                sp.dma_start(x_all[:, lo:hi, :], x[lo * P:hi * P, :].rearrange("(t p) f -> p t f", p=P)
                             ).then_inc(x_loaded[k], 16)

            def load_unit(i, u):
                sp.dma_start(adj_buf[:, u, :], adj[bass.ds((i * BATCH + u // HALVES) * P, P),
                                                   u % HALVES * HALF:(u % HALVES + 1) * HALF]).then_inc(adj_loaded[u], 16)

            def load_batch(i):
                for u in range(UNITS):
                    sp.wait_ge(mask_ready, (i - 1) * UNITS + u + 1)
                    load_unit(i, u)

            def store_batch(i, group):
                sp.wait_ge(out_ready, i + 1)
                sp.dma_start(out[bass.ds(i * (BATCH * P), BATCH * P), :].rearrange("(b p) f -> p b f", p=P),
                             x_all[:, bass.ds(i * BATCH, BATCH), :]).then_inc(out_stored[group], 16)

            for u in range(UNITS):
                load_unit(0, u)
            for k in range(4):
                sp.wait_ge(rows_ready, (k + 1) * (FOURS // 4))
                sp.dma_start(table[k * QUARTER * P:(k + 1) * QUARTER * P, :].rearrange("(t p) n -> p t n", p=P),
                             rows_all[:, k * QUARTER:(k + 1) * QUARTER, :]).then_inc(rows_stored[k], 16)
            with sp.Fori(1, STORE_LAG) as i:
                load_batch(i)
            with sp.Fori(STORE_LAG, GROUP_BATCHES + STORE_LAG) as i:
                load_batch(i)
                store_batch(i - STORE_LAG, 0)
            with sp.Fori(GROUP_BATCHES + STORE_LAG, BATCHES) as i:
                load_batch(i)
                store_batch(i - STORE_LAG, 1)
            for i in range(BATCHES - STORE_LAG, BATCHES):
                store_batch(i, 1)

            for g in range(GROUPS):
                sp.wait_ge(out_stored[g], 16 * GROUP_BATCHES)
            sp.wait_ge(w_stored, 16 * GROUPS)
            sp.wait_ge(verdict, 1)
            unfit_nodes = sp.value_load(unfit_n[0:1, 0:1], min_val=0, max_val=N)
            with sp.If(unfit_nodes > 0):
                sp.nop().then_inc(dn_out, 16)
                with sp.Fori(0, TILES) as t:
                    sp.wait_ge(dn_o, t + 1)
                    sp.dma_start(dense_adj, adj[bass.ts(t, P), :]).then_inc(dn_adj, 16)
                    sp.dma_start(x_row, x[bass.ts(t, P), :]).then_inc(dn_x, 16)
                    with sp.Fori(0, TILES // 4) as j:
                        sp.wait_ge(dn_mm, t * (TILES // 4) + j + 1)
                        sp.dma_start(h_blk, table[bass.ts(j, 4 * P), 0:F].rearrange("(b p) f -> p b f", p=P)).then_inc(dn_h, 16)
                    sp.wait_ge(dn_o, t + 2)
                    sp.dma_start(out[bass.ts(t, P), :], o_row).then_inc(dn_out, 16)
                sp.wait_ge(dn_out, 16 * (TILES + 1))

        @block.gpsimd
        def _(pool):
            nc.gpsimd.iota(diff, [[1, P]], base=0, channel_multiplier=-1).then_inc(iotas, 1)
            nc.gpsimd.iota(column, [[1, P]], base=1, channel_multiplier=0).then_inc(iotas, 1)
            nc.gpsimd.iota(node0[:], [[P, BATCH]], base=0, channel_multiplier=1).then_inc(iotas, 1)
            nc.gpsimd.iota(key_parts[:, 0, :], [[0, 2], [1, 256]], base=0, channel_multiplier=0).then_inc(iotas, 1)
            nc.gpsimd.iota(key_parts[:, 1, :], [[1, 2], [0, 256]], base=0, channel_multiplier=0).then_inc(iotas, 1)
            nc.gpsimd.memset(w_x[:], 0.0).then_inc(iotas, 1)
            nc.gpsimd.memset(pool_fence[:], 0.0).then_inc(pool_step, 1)
            def normalize(g, par):
                pool.wait_ge(rstd_ready, stat_group(g * FOUR) + 1)
                if g >= 2:
                    pool.wait_ge(transposed, g - 1)
                for b in (2, 3):
                    t = g * FOUR + b
                    ins = nc.gpsimd.tensor_scalar(normed[par][:, b], x_all[:, t, :], mv_all[:, t, 0:1], rstd[:, t:t + 1],
                                                  ALU.subtract, ALU.mult)
                ins.then_inc(normed_pool, 1)

            for g in range(FOURS):
                normalize(g, g % 2)
            pool.wait_ge(rows_ready, FOURS)
            nc.gpsimd.tensor_copy(sd_all[:], rows_all[:, :, S_COL:ROW]).then_inc(sd_ready, 1)
            for k in range(4):
                pool.wait_ge(rows_stored[k], 16)
            pool.wait_ge(sd_ready, 1)

            def gather_tile(buf, b):
                for k in range(SLOTS):
                    nc.gpsimd.indirect_dma_start(
                        g_view[buf][:, b, k, :], None, table, bass.IndirectOffsetOnAxis(index[:, buf, b, k:k + 1], 0),
                        bounds_check=N - 1, oob_is_err=False).then_inc(gathers_done[buf], 16)

            def gather_batches(q, first=False, last=False):
                for buf in range(BUFS):
                    i = BUFS * q + buf
                    if not first:
                        pool.wait_ge(out_ready, i - BUFS + 1)
                    pool.wait_ge(index_ready, i + 1)
                    pool.wait_ge(pool_step, i + 1)
                    nc.gpsimd.tensor_tensor(pool_fence[:], pool_fence[:], pool_fence[:], ALU.add).then_inc(pool_step, 1)
                    gather_tile(buf, 0)
                    if last and buf == BUFS - 1:
                        pool.wait_ge(index_ready, i + 2)
                    gather_tile(buf, 1)

            def wide_gather(g):
                pool.wait_ge(w_index_ready, g + 1)
                for k in range(WIDE):
                    nc.gpsimd.indirect_dma_start(
                        w_gathered[:, k, :], None, table, bass.IndirectOffsetOnAxis(w_index[:, k:k + 1], 0),
                        bounds_check=N - 1, oob_is_err=False).then_inc(w_gathers, 16)
                nc.gpsimd.indirect_dma_start(
                    w_x[:], None, x, bass.IndirectOffsetOnAxis(w_index[:, WIDE:WIDE + 1], 0),
                    bounds_check=N - 1, oob_is_err=False).then_inc(w_gathers, 16)

            def wide_store(g):
                pool.wait_ge(out_stored[g], 16 * GROUP_BATCHES)
                pool.wait_ge(w_out_ready, g + 1)
                nc.gpsimd.indirect_dma_start(
                    out, bass.IndirectOffsetOnAxis(w_index[:, WIDE:WIDE + 1], 0), w_x[:], None,
                    bounds_check=N - 1, oob_is_err=False).then_inc(w_stored, 16)

            gather_batches(0, first=True)
            with pool.Fori(1, GROUP_ROUNDS) as q:
                gather_batches(q)
            wide_gather(0)
            with pool.Fori(GROUP_ROUNDS, ROUNDS - 1) as q:
                gather_batches(q)
            wide_store(0)
            gather_batches(ROUNDS - 1, last=True)
            wide_gather(1)
            wide_store(1)

        @block.scalar
        def _(act):
            act.dma_start(w_ext[:, 0:F], W).then_inc(w_loaded, 16)
            for k in (0, 1):
                act.dma_start(a_sb[:, k:k + 1], a[k * F:(k + 1) * F, :]).then_inc(a_loaded, 16)
            act.wait_ge(w_transposed, 1)
            nc.scalar.copy(w_t, banks[:, 6, 0:P]).then_inc(w_copied, 1)
            act.wait_ge(wa_made, 1)
            nc.scalar.copy(w_ext[:, S_COL:ROW], banks[:, 7, 0:2]).then_inc(w_ready, 1)

            def normalize(g, par):
                act.wait_ge(rstd_ready, stat_group(g * FOUR) + 1)
                if g >= 2:
                    act.wait_ge(transposed, g - 1)
                for b in (0, 1):
                    t = g * FOUR + b
                    ins = nc.scalar.activation(normed[par][:, b], x_all[:, t, :], ACT.Identity,
                                               bias=nbias[:, t:t + 1], scale=rstd[:, t:t + 1])
                ins.then_inc(normed_act, 1)

            def relu_rows(g, par):
                act.wait_ge(transposed, g + 1)
                if g >= 2:
                    act.wait_ge(projected, g - 1)
                nc.scalar.activation(relu_t[par].rearrange("p b f -> p (b f)"), banks[:, par, :], ACT.Relu,
                                     accum_out=r_sums[:, g:g + 1]).then_inc(relu_ready, 1)

            def take_rows(g, par):
                act.wait_ge(projected, g + 1)
                nc.scalar.copy(rows_all[:, g * FOUR:(g + 1) * FOUR, :].rearrange("p (u w) n -> p u (w n)", u=2),
                               banks[:, 2 + 2 * par:4 + 2 * par, 0:2 * ROW]).then_inc(rows_ready, 1)

            normalize(0, 0)
            for g in range(FOURS):
                if g + 1 < FOURS:
                    normalize(g + 1, (g + 1) % 2)
                relu_rows(g, g % 2)
                if g:
                    take_rows(g - 1, (g - 1) % 2)
            take_rows(FOURS - 1, (FOURS - 1) % 2)

            def mask(i, u):
                act.wait_ge(adj_loaded[u], 16 * i + 16)
                if not starts_int(i):
                    act.wait_ge(half_packed, (i - 1) * UNITS + u + 1)
                nc.scalar.activation(mask_buf[:, u], adj_buf[:, u], ACT.Sign, bias=minus_half[:]).then_inc(mask_ready, 1)

            def softmax(i):
                act.wait_ge(logits_ready, i + 1)
                nc.scalar.activation(prob[:], e2[:], ACT.Exp).then_inc(exp_ready, 1)

            def batch(i, exp=True):
                mask(i, 0)
                if exp:
                    softmax(i - 1 - LAG)
                for u in range(1, UNITS):
                    mask(i, u)

            def wide_softmax(g):
                act.wait_ge(w_logits, g + 1)
                nc.scalar.activation(w_tmp[:, 2], w_tmp[:, 0], ACT.Exp, bias=w_m[:, 0:1], accum_out=w_m[:, 1:2]
                                     ).then_inc(w_exp, 1)

            for i in range(1 + LAG):
                batch(i, exp=False)
            with act.Fori(1 + LAG, GROUP_BATCHES + 1 + BUFS) as i:
                batch(i)
            wide_softmax(0)
            with act.Fori(GROUP_BATCHES + 1 + BUFS, BATCHES) as i:
                batch(i)
            for i in range(BATCHES - 1 - LAG, BATCHES):
                softmax(i)
            wide_softmax(1)

            act.wait_ge(verdict, 1)
            unfit_nodes = act.value_load(unfit_n[0:1, 0:1], min_val=0, max_val=N)
            with act.If(unfit_nodes > 0):
                act.nop().then_inc(dn_pt, 1)
                with act.Fori(0, TILES) as t:
                    act.wait_ge(dn_max, t + 1)
                    nc.scalar.activation(dense_e, dense_e, ACT.Exp, bias=cols[:, 0:1], accum_out=cols[:, 1:2]
                                         ).then_inc(dn_exp, 1)
                    act.wait_ge(dn_exp, t + 1)
                    with act.Fori(0, TILES // 4) as j:
                        act.wait_ge(dn_tr, t * (TILES // 4) + j + 1)
                        nc.scalar.copy(e_blk, dense_e[:, bass.ds(j * (4 * P), 4 * P)].rearrange("p (b f) -> p b f", b=4)
                                       ).then_inc(dn_blk, 1)
                        act.wait_ge(dn_tr, t * (TILES // 4) + j + 2)
                        act.wait_ge(dn_mm, t * (TILES // 4) + j + 1)
                        nc.scalar.copy(p_t, banks[:, 4, :].rearrange("p (b f) -> p b f", b=4)).then_inc(dn_pt, 1)

        @block.vector
        def _(dve):
            done = Count(dve_step)

            def settled():
                dve.wait_ge(dve_step, done.value())

            def fenced():
                settled()
                done.add(nc.vector.memset(fence[:], 0.0))

            v = nc.vector
            done.add(v.memset(ones[:], 1.0))
            done.add(v.memset(ones_b[:], 1.0))
            done.add(v.memset(zeros[:], 0.0))
            done.add(v.memset(wide_base[:], 1.0))
            done.add(v.memset(node_base[:], 0.0))
            done.add(v.memset(unfit_all[:], 0.0))
            done.add(v.memset(minus_half[:], -0.5))
            dve.wait_ge(iotas, 6)
            done.add(v.tensor_scalar(ident[:], diff, 0.0, None, ALU.is_equal))
            done.add(v.tensor_scalar(before[:], diff, 0.0, None, ALU.is_gt))
            done.add(v.tensor_copy(column_1[:], column))
            settled()
            v.memset(rec[:], 1.0).then_inc(const_made, 1)

            def statistics(k):
                lo, hi = STAT_GROUPS[k]
                dve.wait_ge(x_loaded[k], 16)
                settled()
                for t in range(lo, hi):
                    done.add(v.bn_stats(stats[:, t - lo], x_all[:, t, :]))
                settled()
                for t in range(lo, hi):
                    done.add(v.bn_aggr(mv_all[:, t, :], stats[:, t - lo]))
                settled()
                done.add(v.tensor_scalar(var_e[:, lo:hi], mv_all[:, lo:hi, 1], EPS, None, ALU.add))
                settled()
                square, factor = newton[:, 0, 0:hi - lo], newton[:, 1, 0:hi - lo]
                done.add(v.tensor_scalar(square.bitcast(i32), var_e[:, lo:hi].bitcast(i32), 1, None, ALU.arith_shift_right))
                settled()
                done.add(v.tensor_scalar(rstd[:, lo:hi].bitcast(i32), square.bitcast(i32), -1.0, float(MAGIC),
                                         ALU.mult, ALU.add))
                for _ in range(NEWTON_STEPS):
                    settled()
                    done.add(v.tensor_tensor(square, rstd[:, lo:hi], rstd[:, lo:hi], ALU.mult))
                    settled()
                    done.add(v.scalar_tensor_tensor(factor, square, -0.5, var_e[:, lo:hi], ALU.mult, ALU.mult))
                    settled()
                    done.add(v.scalar_tensor_tensor(rstd[:, lo:hi], factor, 1.5, rstd[:, lo:hi], ALU.add, ALU.mult))
                settled()
                v.scalar_tensor_tensor(nbias[:, lo:hi], mv_all[:, lo:hi, 0], -1.0, rstd[:, lo:hi], ALU.mult, ALU.mult
                                       ).then_inc(rstd_ready, 1)

            for k in range(len(STAT_GROUPS)):
                statistics(k)

            for c in range(BITS):
                done.add(v.tensor_scalar(bit_ident[:, c], ident[:], float(1 << c) / 2, None, ALU.mult))
            done.add(v.tensor_scalar(key_tmp, key_parts[:, 0], ident[:, 0:1], 1.0 / BIT_COLS, ALU.mult, ALU.mult))
            settled()
            done.add(v.tensor_scalar(rest[:], key_parts[:, 1], ident[:, 1:2], 256.0 / BIT_COLS, ALU.mult, ALU.mult))
            settled()
            done.add(v.tensor_tensor(key_tmp, key_tmp, rest[:], ALU.add))
            settled()
            done.add(v.tensor_scalar(fence[:], ident[:, 2:3], -0.5, None, ALU.mult))
            settled()
            v.tensor_scalar(key_rows[:], key_tmp, fence[:, 0:1], None, ALU.add).then_inc(keys_made, 1)
            dve.wait_ge(relu_ready, FOURS)
            done.add(v.tensor_reduce(r_sum[:], r_sums[:], AX.X, ALU.add))
            settled()
            v.tensor_scalar(r_sum_cols[:], ones[:], r_sum[:, 0:1], None, ALU.mult).then_inc(r_summed, 1)
            dve.wait_ge(mean_ready, 1)
            done.add(v.tensor_scalar(mean_h[:], banks[:, 0, 0:F], 1.0 / N, None, ALU.mult))
            dve.wait_ge(keys_made, 1)
            dve.wait_ge(w_ready, 1)
            done.add(v.memset(w_gathered[:], 0.0))
            dve.wait_ge(sd_ready, 1)

            def first_words(b):
                done.add(v.max(words[:, b, 0:8], banks[:, 6 + b]))

            def remove_words(b):
                v.match_replace(rest[:], words[:, b, 0:8], banks[:, 6 + b], -float(1 << BITS)).then_inc(words_read, 1)

            def second_words(b):
                done.add(v.max(words[:, b, 8:16], rest[:]))

            def decode(par, lo=0, hi=BATCH):
                B = slice(lo, hi)
                done.add(v.tensor_scalar(wi[0][:, B], words[:, B], float(BIT_COLS), None, ALU.mult))
                settled()
                done.add(v.tensor_scalar(wi[1][:, B], wi[0][:, B], BIT_COLS - 1, None, ALU.bitwise_and))
                done.add(v.tensor_scalar(wi[2][:, B], wi[0][:, B], 9, None, ALU.arith_shift_right))
                settled()
                done.add(v.tensor_scalar(wf[0][:, B], wi[2][:, B], float(1 << (BITS - 1)), None, ALU.add))
                settled()
                done.add(v.tensor_scalar(wi[0][:, B], wf[0][:, B].bitcast(i32), 23, None, ALU.logical_shift_right))
                done.add(v.tensor_scalar(top_bit[:, B], wf[0][:, B].bitcast(i32), 0x7F800000, None, ALU.bitwise_and))
                settled()
                done.add(v.scalar_tensor_tensor(cand[:, B, 0:WIDE], wi[0][:, B], float(BIT_COLS), wi[1][:, B], ALU.mult, ALU.add))
                done.add(v.tensor_tensor(wf[1][:, B], wf[0][:, B], top_bit[:, B].bitcast(f32), ALU.subtract))
                settled()
                done.add(v.tensor_scalar(wi[2][:, B], wf[1][:, B].bitcast(i32), 23, None, ALU.logical_shift_right))
                done.add(v.tensor_scalar(top_bit[:, B], wf[1][:, B].bitcast(i32), 0x7F800000, None, ALU.bitwise_and))
                settled()
                done.add(v.scalar_tensor_tensor(cand[:, B, WIDE:], wi[2][:, B], float(BIT_COLS), wi[1][:, B], ALU.mult, ALU.add))
                done.add(v.tensor_tensor(wf[2][:, B], wf[1][:, B], top_bit[:, B].bitcast(f32), ALU.subtract))
                settled()
                done.add(v.tensor_reduce(unfit[:, 0, B], wf[2][:, B], AX.X, ALU.max))
                done.add(v.tensor_copy(unfit[:, 1, B], wf[0][:, B, WIDE - 1]))
                settled()
                done.add(v.tensor_scalar(cand_half[:, B], cand[:, B], float(EXP_BIAS), 0.5, ALU.is_ge, ALU.subtract))
                settled()
                done.add(v.tensor_reduce(unfit[:, 2, B], cand_half[:, B], AX.X, ALU.add))
                for b in range(lo, hi):
                    done.add(v.max(top[:, b, 0:8], cand[:, b]))
                fenced()
                for b in range(lo, hi):
                    done.add(v.match_replace(cand[:, b], top[:, b, 0:8], cand[:, b], 0.0))
                fenced()
                for b in range(lo, hi):
                    done.add(v.max(top[:, b, 8:16], cand[:, b]))
                settled()
                done.add(v.tensor_scalar(skip[:, B], top[:, B, 0:SLOTS], float(EXP_BIAS), SKIP, ALU.is_lt, ALU.mult))
                done.add(v.tensor_scalar(valid[:, par, B], top[:, B, 0:SLOTS], float(EXP_BIAS), None, ALU.is_ge))
                settled()
                v.scalar_tensor_tensor(index[:, par, B], top[:, B, 0:SLOTS], -float(EXP_BIAS), skip[:, B],
                                       ALU.add, ALU.add).then_inc(index_ready, 1)
                done.add(v.tensor_scalar(masked[:, par, B], valid[:, par, B], 1.0, MASKED, ALU.subtract, ALU.mult))

            def make_records(i):
                if not starts_int(i):
                    dve.wait_ge(records_added, i)
                done.add(v.tensor_copy(rec[:, :, 0:WIDE], top[:]))
                done.add(v.tensor_copy(rec[:, :, REC_S], sd_all[:, bass.ds(i * BATCH, BATCH), 0]))
                done.add(v.tensor_scalar(rec[:, :, REC_NODE], node0[:], node_base[:, 0:1], None, ALU.add))
                settled()
                done.add(v.tensor_scalar(node_base[:], node_base[:], float(BATCH * P), None, ALU.add))
                v.tensor_scalar(is_wide[:], top[:, :, SLOTS], float(EXP_BIAS), None, ALU.is_ge).then_inc(wide_flagged, 1)

            def place_wide(i):
                dve.wait_ge(prefix_ready, i + 1)
                done.add(v.scalar_tensor_tensor(pos[:], banks[:, 2, 0:BATCH], wide_base[:, 0:1], is_wide[:], ALU.add, ALU.mult))
                settled()
                done.add(v.tensor_tensor(wide_base[:], wide_base[:], banks[:, 2, BATCH:BATCH + 1], ALU.add))
                done.add(v.tensor_scalar(unfit[:, 3], pos[:], float(P), None, ALU.subtract))
                for b in range(BATCH):
                    ins = v.tensor_scalar(one_hot[:, b], column_1[:], pos[:, b:b + 1], None, ALU.is_equal)
                ins.then_inc(one_hot_ready, 1)
                settled()
                done.add(v.tensor_reduce(unfit_top[:], unfit[:], AX.XY, ALU.max))
                settled()
                done.add(v.tensor_tensor(unfit_all[:], unfit_all[:], unfit_top[:], ALU.max))

            def logits(i, par, gathered_times):
                d = g_view[par][:, :, :, D_COL]
                s = sd_all[:, bass.ds(i * BATCH, BATCH), 0:1].to_broadcast([P, BATCH, SLOTS])
                dve.wait_ge(gathers_done[par], 16 * BATCH * SLOTS * gathered_times)
                settled()
                done.add(v.tensor_tensor(e[:], d, s, ALU.add))
                settled()
                done.add(v.scalar_tensor_tensor(e2[:], e[:], ALPHA, e[:], ALU.mult, ALU.max))
                settled()
                done.add(v.tensor_tensor(e[:], e2[:], valid[:, par], ALU.mult))
                settled()
                done.add(v.tensor_tensor(e[:], e[:], masked[:, par], ALU.add))
                settled()
                done.add(v.tensor_reduce(m4[:], e[:], AX.X, ALU.max))
                settled()
                v.tensor_tensor(e2[:], e[:], m4[:].unsqueeze(2).to_broadcast([P, BATCH, SLOTS]), ALU.subtract
                                ).then_inc(logits_ready, 1)

            def weighted_sum(i, par, gathered_times):
                dve.wait_ge(exp_ready, i + 1)
                done.add(v.tensor_tensor(weight[:], prob[:], valid[:, par], ALU.mult))
                settled()
                done.add(v.tensor_reduce(l4[:], weight[:], AX.X, ALU.add))
                settled()
                done.add(v.tensor_scalar(alone[:], l4[:], 0.5, None, ALU.is_lt))
                done.add(v.tensor_scalar(m4[:], l4[:], 0.5, None, ALU.max))
                settled()
                done.add(v.reciprocal(l4[:], m4[:]))
                settled()
                done.add(v.tensor_tensor(weight[:], weight[:], l4[:].unsqueeze(2).to_broadcast([P, BATCH, SLOTS]), ALU.mult))
                at = [x_all[:, bass.ds(i * BATCH + b, 1), :].rearrange("p a f -> p (a f)") for b in range(BATCH)]
                for b in range(BATCH):
                    done.add(v.scalar_tensor_tensor(at[b], mean_h[:], alone[:, b:b + 1], at[b], ALU.mult, ALU.add))
                for k in range(SLOTS):
                    settled()
                    for b in range(BATCH):
                        ins = v.scalar_tensor_tensor(at[b], g_view[par][:, b, k, 0:F], weight[:, b, k:k + 1], at[b],
                                                     ALU.mult, ALU.add)
                        if k < SLOTS - 1 or b < BATCH - 1:
                            done.add(ins)
                ins.then_inc(out_ready, 1)

            def step(q, buf, lagging):
                i = BUFS * q + buf
                dve.wait_ge(half_packed, i * UNITS + HALVES)
                fenced()
                first_words(0)
                if lagging:
                    logits(i - LAG, (buf - LAG) % BUFS, q + (buf >= LAG))
                fenced()
                remove_words(0)
                dve.wait_ge(words_read, i * BATCH + 1)
                dve.wait_ge(half_packed, i * UNITS + UNITS)
                fenced()
                second_words(0)
                first_words(1)
                fenced()
                remove_words(1)
                dve.wait_ge(words_read, i * BATCH + 2)
                fenced()
                second_words(1)
                settled()
                decode(buf)
                make_records(i)
                if lagging:
                    weighted_sum(i - LAG, (buf - LAG) % BUFS, q + (buf >= LAG))
                place_wide(i)

            def last_step(i):
                dve.wait_ge(half_packed, i * UNITS + HALVES)
                fenced()
                first_words(0)
                fenced()
                remove_words(0)
                dve.wait_ge(words_read, i * BATCH + 1)
                fenced()
                second_words(0)
                settled()
                decode(i % BUFS, 0, 1)
                logits(i - LAG, (i - LAG) % BUFS, (i - LAG) // BUFS + 1)
                dve.wait_ge(half_packed, i * UNITS + UNITS)
                fenced()
                first_words(1)
                fenced()
                remove_words(1)
                dve.wait_ge(words_read, i * BATCH + 2)
                fenced()
                second_words(1)
                settled()
                decode(i % BUFS, 1, 2)
                make_records(i)
                weighted_sum(i - LAG, (i - LAG) % BUFS, (i - LAG) // BUFS + 1)
                place_wide(i)

            def main_round(q, first=False):
                for buf in range(BUFS):
                    step(q, buf, not (first and buf < LAG))

            def wide_index(g):
                dve.wait_ge(records_closed, g + 1)
                if g:
                    dve.wait_ge(w_stored, 16 * g)
                settled()
                v.tensor_copy(w_rec[:], banks[:, 3, 0:REC]).then_inc(records_read, 1)
                dve.wait_ge(records_read, g + 1)
                done.add(v.tensor_scalar(w_tmp[:, 0], w_rec[:, 0:WIDE], float(EXP_BIAS), SKIP, ALU.is_lt, ALU.mult))
                done.add(v.tensor_scalar(w_valid[:], w_rec[:, 0:WIDE], float(EXP_BIAS), None, ALU.is_ge))
                done.add(v.tensor_scalar(w_m[:, 0:1], w_rec[:, REC_ONE:REC_ONE + 1], -SKIP, SKIP, ALU.mult, ALU.add))
                settled()
                done.add(v.scalar_tensor_tensor(w_index[:, 0:WIDE], w_rec[:, 0:WIDE], -float(EXP_BIAS), w_tmp[:, 0],
                                                ALU.add, ALU.add))
                settled()
                v.tensor_tensor(w_index[:, WIDE:WIDE + 1], w_rec[:, REC_NODE:REC_NODE + 1], w_m[:, 0:1], ALU.add
                                ).then_inc(w_index_ready, 1)

            def wide_sum(g):
                dve.wait_ge(w_gathers, 16 * (WIDE + 1) * (g + 1))
                settled()
                done.add(v.tensor_scalar(w_tmp[:, 0], w_gathered[:, :, D_COL], w_rec[:, REC_S:REC_S + 1], None, ALU.add))
                settled()
                done.add(v.scalar_tensor_tensor(w_tmp[:, 1], w_tmp[:, 0], ALPHA, w_tmp[:, 0], ALU.mult, ALU.max))
                settled()
                done.add(v.tensor_tensor(w_tmp[:, 0], w_tmp[:, 1], w_valid[:], ALU.mult))
                settled()
                done.add(v.tensor_scalar(w_tmp[:, 1], w_valid[:], 1.0, MASKED, ALU.subtract, ALU.mult))
                settled()
                done.add(v.tensor_tensor(w_tmp[:, 0], w_tmp[:, 0], w_tmp[:, 1], ALU.add))
                settled()
                v.tensor_reduce(w_m[:, 0:1], w_tmp[:, 0], AX.X, ALU.max, negate=True).then_inc(w_logits, 1)
                dve.wait_ge(w_exp, g + 1)
                done.add(v.reciprocal(w_m[:, 1:2], w_m[:, 1:2]))
                settled()
                done.add(v.tensor_scalar(w_tmp[:, 2], w_tmp[:, 2], w_m[:, 1:2], None, ALU.mult))
                for k in range(WIDE):
                    settled()
                    ins = v.scalar_tensor_tensor(w_x[:], w_gathered[:, k, 0:F], w_tmp[:, 2, k:k + 1], w_x[:], ALU.mult, ALU.add)
                    if k < WIDE - 1:
                        done.add(ins)
                ins.then_inc(w_out_ready, 1)


            def main_rounds(lo, hi):
                with dve.Fori(lo, hi) as q:
                    done.enter(q - lo, BUFS * DVE_STEPS)
                    main_round(q)
                    done.leave(hi - lo)

            main_round(0, first=True)
            main_rounds(1, GROUP_ROUNDS)
            wide_index(0)
            done.add(v.memset(wide_base[:], 1.0))
            main_round(GROUP_ROUNDS)
            wide_sum(0)
            main_rounds(GROUP_ROUNDS + 1, ROUNDS - 1)
            for buf in range(BUFS - 1):
                step(ROUNDS - 1, buf, True)
            last_step(BATCHES - 1)
            wide_index(1)
            for i in range(BATCHES - LAG, BATCHES):
                logits(i, i % BUFS, ROUNDS)
                weighted_sum(i, i % BUFS, ROUNDS)
            wide_sum(1)

            settled()
            v.tensor_scalar(unfit_top[:], unfit_all[:], 0.0, None, ALU.is_gt).then_inc(unfit_ready, 1)
            dve.wait_ge(unfit_summed, 1)
            v.tensor_copy(unfit_n[:], banks[:, 4, 0:1]).then_inc(verdict, 1)
            dve.wait_ge(verdict, 1)
            unfit_nodes = dve.value_load(unfit_n[0:1, 0:1], min_val=0, max_val=N)
            with dve.If(unfit_nodes > 0):
                dve.nop().then_inc(dn_row, 1)
                dve.nop().then_inc(dn_o, 1)
                dve.nop().then_inc(dn_step, 1)
                with dve.Fori(0, TILES) as j:
                    dve.wait_ge(dn_bcast, j + 1)
                    v.tensor_scalar(d_diag, ident[:], sd_all[:, j, 1:2], None, ALU.mult).then_inc(dn_diag, 1)
                    dve.wait_ge(dn_bcast, j + 2)
                    v.tensor_copy(dense_d[:, bass.ds(j * P, P)], banks[:, 4, 0:P]).then_inc(dn_row, 1)
                dve.wait_ge(dn_row, TILES + 1)
                v.memset(d_diag, 0.0).then_inc(dn_row, 1)
                with dve.Fori(0, TILES) as t:
                    dense = Count(dn_step, credit=1)
                    dense.enter(t, 8)

                    def dense_settled():
                        dve.wait_ge(dn_step, dense.value())

                    dve.wait_ge(dn_adj, 16 * t + 16)
                    dve.wait_ge(dn_tr, t * (TILES // 4) + 1)
                    dense.add(v.tensor_scalar(dense_e, dense_d, sd_all[:, t, 0:1], None, ALU.add))
                    dense.add(v.tensor_scalar(dense_m, dense_adj, 0.0, None, ALU.is_gt))
                    dense_settled()
                    dense.add(v.scalar_tensor_tensor(dense_e, dense_e, ALPHA, dense_e, ALU.mult, ALU.max))
                    dense_settled()
                    dense.add(v.tensor_tensor(dense_e, dense_e, dense_m, ALU.mult))
                    dense_settled()
                    dense.add(v.tensor_scalar(dense_m, dense_m, 1.0, MASKED, ALU.subtract, ALU.mult))
                    dense_settled()
                    dense.add(v.tensor_tensor(dense_e, dense_e, dense_m, ALU.add))
                    dense_settled()
                    v.tensor_reduce(cols[:, 0:1], dense_e, AX.X, ALU.max, negate=True).then_inc(dn_max, 1)
                    dve.wait_ge(dn_exp, t + 1)
                    dense.add(v.reciprocal(cols[:, 2:3], cols[:, 1:2]))
                    dense_settled()
                    dve.wait_ge(dn_sum, t + 1)
                    dve.wait_ge(dn_x, 16 * t + 16)
                    dve.wait_ge(dn_out, 16 * t + 16)
                    v.scalar_tensor_tensor(o_row, banks[:, 5, 0:F], cols[:, 2:3], x_row, ALU.mult, ALU.add).then_inc(dn_o, 1)
                    dense.add(v.memset(fence[:], 0.0))

        @block.tensor
        def _(pe):
            mm = nc.tensor.matmul
            pe.wait_ge(const_made, 1)
            pe.wait_ge(w_loaded, 16)
            nc.tensor.transpose(banks[:, 6, 0:P], w_ext[:, 0:F], ident[:]).then_inc(w_transposed, 1)
            pe.wait_ge(w_copied, 1)
            pe.wait_ge(a_loaded, 32)
            mm(banks[:, 7, 0:2], w_t, a_sb[:], start=True, stop=True).then_inc(wa_made, 1)
            pe.wait_ge(w_ready, 1)

            def transpose_rows(g, par):
                pe.wait_ge(normed_act, g + 1)
                pe.wait_ge(normed_pool, g + 1)
                if not starts(g):
                    pe.wait_ge(relu_ready, g - 1)
                for b in range(FOUR):
                    ins = nc.tensor.transpose(banks[:, par, b * P:(b + 1) * P], normed[par][:, b], ident[:])
                ins.then_inc(transposed, 1)

            def project(g, par):
                pe.wait_ge(relu_ready, g + 1)
                if not starts(g):
                    pe.wait_ge(rows_ready, g - 1)
                for b in range(FOUR):
                    at = b % 2 * ROW
                    ins = mm(banks[:, 2 + 2 * par + b // 2, at:at + ROW], relu_t[par][:, b], w_ext[:], start=True, stop=True)
                ins.then_inc(projected, 1)

            def project_pair(q, last=False):
                transpose_rows(2 * q + 1, 1)
                project(2 * q, 0)
                if not last:
                    transpose_rows(2 * q + 2, 0)
                project(2 * q + 1, 1)

            transpose_rows(0, 0)
            project_pair(0)
            with pe.Fori(1, FOURS // 2 - 1) as q:
                project_pair(q)
            project_pair(FOURS // 2 - 1, last=True)
            pe.wait_ge(r_summed, 1)
            mm(banks[:, 0, 0:F], r_sum_cols[:], w_ext[:, 0:F], start=True, stop=True).then_inc(mean_ready, 1)
            pe.wait_ge(rows_ready, FOURS)
            pe.wait_ge(keys_made, 1)

            def pack(i, u):
                b, h = u // HALVES, u % HALVES
                pe.wait_ge(mask_ready, i * UNITS + u + 1)
                if h == 0:
                    if not starts_int(i):
                        pe.wait_ge(words_read, (i - 1) * BATCH + b + 1)
                    mm(banks[:, 6 + b], ones_b[0:3, :], key_rows[0:3, :], start=True, stop=False)
                for c in range(HALF_BITS):
                    ins = mm(banks[:, 6 + b], bit_ident[:, h * HALF_BITS + c], mask_buf[:, u, c * BIT_COLS:(c + 1) * BIT_COLS],
                             start=False, stop=(h == 1 and c == HALF_BITS - 1))
                ins.then_inc(half_packed, 1)

            def count_wide(i):
                pe.wait_ge(wide_flagged, i + 1)
                if not starts_int(i):
                    pe.wait_ge(one_hot_ready, i)
                for b in range(BATCH):
                    mm(banks[:, 2, b:b + 1], before[:], is_wide[:, b:b + 1], start=True, stop=(b == 0))
                    for c in range(b):
                        mm(banks[:, 2, b:b + 1], ones_b[:], is_wide[:, c:c + 1], start=False, stop=(c == b - 1))
                for b in range(BATCH):
                    ins = mm(banks[:, 2, BATCH:BATCH + 1], ones_b[:], is_wide[:, b:b + 1], start=(b == 0), stop=(b == BATCH - 1))
                ins.then_inc(prefix_ready, 1)

            def add_records(i):
                pe.wait_ge(one_hot_ready, i + 1)
                for b in range(BATCH):
                    ins = mm(banks[:, 3, 0:REC], one_hot[:, b], rec[:, b], start=False, stop=False)
                ins.then_inc(records_added, 1)

            def batch(i):
                pack(i, 0)
                count_wide(i - 1)
                for u in range(1, UNITS):
                    pack(i, u)
                add_records(i - 1)

            def open_records():
                mm(banks[:, 3, 0:REC], ones[:], zeros[:, 0:REC], start=True, stop=False)

            def close_records():
                mm(banks[:, 3, 0:REC], ones[:], zeros[:, 0:REC], start=False, stop=True).then_inc(records_closed, 1)

            for u in range(UNITS):
                pack(0, u)
            open_records()
            batch(1)
            with pe.Fori(2, GROUP_BATCHES) as i:
                batch(i)
            i = GROUP_BATCHES
            pack(i, 0)
            count_wide(i - 1)
            add_records(i - 1)
            close_records()
            for u in range(1, UNITS):
                pack(i, u)
            pe.wait_ge(records_read, 1)
            open_records()
            with pe.Fori(GROUP_BATCHES + 1, BATCHES) as i:
                batch(i)
            count_wide(BATCHES - 1)
            add_records(BATCHES - 1)
            close_records()
            pe.wait_ge(unfit_ready, 1)
            mm(banks[:, 4, 0:1], ones[:], unfit_top[:], start=True, stop=True).then_inc(unfit_summed, 1)

            pe.wait_ge(verdict, 1)
            unfit_nodes = pe.value_load(unfit_n[0:1, 0:1], min_val=0, max_val=N)
            with pe.If(unfit_nodes > 0):
                pe.nop().then_inc(dn_bcast, 1)
                pe.nop().then_inc(dn_tr, 1)
                pe.nop().then_inc(dn_mm, 1)
                with pe.Fori(0, TILES) as j:
                    pe.wait_ge(dn_diag, j + 1)
                    pe.wait_ge(dn_row, j + 1)
                    mm(banks[:, 4, 0:P], ones[:], d_diag, start=True, stop=True).then_inc(dn_bcast, 1)
                pe.wait_ge(dn_row, TILES + 2)
                with pe.Fori(0, TILES) as t:
                    pe.wait_ge(dn_o, t + 1)
                    mm(banks[:, 5, 0:F], ones[:], d_diag, start=True, stop=False)
                    with pe.Fori(0, TILES // 4) as j:
                        at = t * (TILES // 4) + j
                        pe.wait_ge(dn_blk, at + 1)
                        pe.wait_ge(dn_pt, at + 1)
                        for b in range(4):
                            ins = nc.tensor.transpose(banks[:, 4, b * P:(b + 1) * P], e_blk[:, b], ident[:])
                        ins.then_inc(dn_tr, 1)
                        pe.wait_ge(dn_pt, at + 2)
                        pe.wait_ge(dn_h, 16 * at + 16)
                        for b in range(4):
                            ins = mm(banks[:, 5, 0:F], p_t[:, b], h_blk[:, b], start=False, stop=False)
                        ins.then_inc(dn_mm, 1)
                    mm(banks[:, 5, 0:F], ones[:], d_diag, start=False, stop=True).then_inc(dn_sum, 1)


def stat_group(t):
    return [t < hi for lo, hi in STAT_GROUPS].index(True)


def starts(g):
    return isinstance(g, int) and g < 2


def starts_int(i):
    return isinstance(i, int) and i == 0


def kernel(**inputs):
    import numpy as np
    import concourse.bacc as bacc
    from concourse.bass_utils import run_bass_kernel_spmd

    nc = bacc.Bacc("TRN2", target_bir_lowering=False, num_devices=1)
    arrays, args = {}, []
    for name in ("x", "adj", "L0_gnn_W", "L0_gnn_a"):
        arrays[f"in_{name}"] = np.ascontiguousarray(inputs[name])
        args.append(nc.dram_tensor(f"in_{name}", arrays[f"in_{name}"].shape,
                                   mybir.dt.from_np(arrays[f"in_{name}"].dtype), kind="ExternalInput").ap())
    args.append(nc.dram_tensor("out", (N, F), mybir.dt.float32, kind="ExternalOutput").ap())
    gat_kernel(nc, *args)
    return run_bass_kernel_spmd(nc, [arrays], core_ids=[0]).results[0]["out"]
```

```python
import concourse.bass as bass
from concourse import mybir
from contextlib import ExitStack

P = 128
N = 8192
F = 128
TILES = N // P
QUARTER = TILES // 4
STAT_GROUPS = [(0, 8), (8, 16), (16, 32), (32, 48), (48, 64)]
FOUR = 4
FOURS = TILES // FOUR
BATCH = 2
BATCHES = TILES // BATCH
EARLY_MASKS = (2, 6)
BUFS = 4
LAG = 2
ROUNDS = BATCHES // BUFS
GROUPS = 2
GROUP_ROUNDS = ROUNDS // GROUPS
GROUP_BATCHES = BATCHES // GROUPS
BIT_COLS = 512
BITS = N // BIT_COLS
PARTS = 4
UNITS = BATCH * PARTS
PART = N // PARTS
PART_BITS = BITS // PARTS
STORE_LAG = 6
SLOTS = 8
WIDE = 16
ROW = F + 2
S_COL, D_COL = F, F + 1
MORE = WIDE - SLOTS
REC = MORE + 4
REC_S, REC_NODE, REC_ONE = MORE, MORE + 1, MORE + 2
SUMS = F + 2
EPS = 1e-5
ALPHA = 0.2
MASKED = 9e15
EXP_BIAS = 127 * BIT_COLS
DVE_STEPS = 73
MAGIC = 0x5F3759DF
NEWTON_STEPS = 3
SKIP = 100000.0


class Count:

    def __init__(self, sem, credit=0):
        self.sem, self.base, self.n, self.total = sem, credit, 0, credit

    def add(self, ins):
        ins.then_inc(self.sem, 1)
        self.n += 1
        return self.value()

    def value(self):
        return self.base + self.n

    def enter(self, i, per):
        self.total += self.n
        self.base, self.n, self.per = i * per + self.total, 0, per

    def leave(self, times):
        assert self.n == self.per, f"{self.n} signals in the loop's body, not {self.per}"
        self.total += times * self.per
        self.base, self.n = self.total, 0


def gat_kernel(nc, x, adj, W, a, out):
    f32, bf16 = mybir.dt.float32, mybir.dt.bfloat16
    i32, u32 = mybir.dt.int32, mybir.dt.uint32
    ALU, ACT, AX = mybir.AluOpType, mybir.ActivationFunctionType, mybir.AxisListType

    table = nc.dram_tensor("table", (N, ROW), f32).ap()

    ctx = ExitStack()
    with ctx:
        def sb(name, shape, dt):
            return ctx.enter_context(nc.sbuf_tensor(name, shape, dt))

        def sem(name):
            return ctx.enter_context(nc.semaphore(name))

        adj_buf = sb("adj_buf", [P, UNITS, PART], i32)
        mask_buf = sb("mask_buf", [P, UNITS, PART], bf16)
        gathered = sb("gathered", [P, BUFS, BATCH * SLOTS * ROW], f32)
        g_view = [gathered[:, buf, :].rearrange("p (b k n) -> p b k n", b=BATCH, k=SLOTS) for buf in range(BUFS)]
        rows_all = gathered[:, :, :].rearrange("p a (t n) -> p (a t) n", n=ROW)
        x_all = sb("x_all", [P, TILES, F], f32)
        work = sb("work", [P, 4, FOUR, F], f32)
        normed, relu_t = [work[:, 0], work[:, 1]], [work[:, 2], work[:, 3]]
        e_blk, p_t = normed[0], relu_t[0]
        h_blk = x_all[:, 0:FOUR, :]
        x_row, o_row, d_diag = normed[1][:, 0, :], normed[1][:, 1, :], normed[1][:, 2, :]
        dense_adj = adj_buf[:, 0:UNITS // 2, :].rearrange("p u n -> p (u n)")
        dense_d = adj_buf[:, UNITS // 2:, :].rearrange("p u n -> p (u n)").bitcast(f32)
        dense_e = mask_buf[:, :, :].rearrange("p u n -> p (u n)").bitcast(f32)
        dense_m = gathered[:, :, :].rearrange("p a n -> p (a n)")[:, 0:N]

        w_ext = sb("w_ext", [P, ROW], f32)
        a_sb = sb("a_sb", [P, 2], f32)
        column_1 = sb("column_1", [P, P], f32)
        node0 = sb("node0", [P, BATCH], i32)
        ident = sb("ident", [P, P], f32)
        ones = sb("ones", [P, P], f32)
        ones_b = sb("ones_b", [P, P], bf16)
        before = sb("before", [P, P], bf16)
        bit_ident = sb("bit_ident", [P, BITS, P], bf16)
        minus_half = sb("minus_half", [P, 1], f32)
        key_rows = sb("key_rows", [P, BIT_COLS], bf16)
        stats = sb("stats", [P, QUARTER, 6], f32)
        mv_all = sb("mv_all", [P, TILES, 2], f32)
        rstd = sb("rstd", [P, TILES], f32)
        nbias = sb("nbias", [P, TILES], f32)
        newton = sb("newton", [P, 2, QUARTER], f32)
        r_sums = sb("r_sums", [P, FOURS], f32)
        r_sum = sb("r_sum", [P, 1], f32)
        r_sum_cols = sb("r_sum_cols", [P, P], f32)
        var_e = sb("var_e", [P, TILES], f32)
        mean_h = sb("mean_h", [P, F], f32)
        sd_all = sb("sd_all", [P, TILES, 2], f32)
        fence = sb("fence", [P, 1], f32)
        pool_fence = sb("pool_fence", [P, 1], f32)
        rest = sb("rest", [P, BIT_COLS], f32)
        words = sb("words", [P, BATCH, WIDE], f32)
        wi = [sb(f"wi{k}", [P, BATCH, WIDE], i32) for k in range(3)]
        wf = [sb(f"wf{k}", [P, BATCH, WIDE], f32) for k in range(3)]
        top_bit = sb("top_bit", [P, BATCH, WIDE], i32)
        cand = sb("cand", [P, BATCH, 2 * WIDE], f32)
        cand_half = sb("cand_half", [P, BATCH, 2 * WIDE], f32)
        node_base = sb("node_base", [P, 1], f32)
        top = sb("top", [P, BATCH, WIDE], f32)
        skip = sb("skip", [P, BATCH, SLOTS], f32)
        index = sb("index", [P, BUFS, BATCH, SLOTS], u32)
        valid = sb("valid", [P, BUFS, BATCH, SLOTS], f32)
        masked = sb("masked", [P, BUFS, BATCH, SLOTS], f32)
        rec = sb("rec", [P, BATCH, REC], f32)
        is_wide = sb("is_wide", [P, BATCH], bf16)
        wide_base = sb("wide_base", [P, 1], f32)
        pos = sb("pos", [P, BATCH], f32)
        one_hot = sb("one_hot", [P, BUFS, BATCH, P], f32)
        max_sum = sb("max_sum", [P, BUFS, BATCH, 2], f32)
        unfit = sb("unfit", [P, 4, BATCH], f32)
        unfit_top = sb("unfit_top", [P, 1], f32)
        zeros = sb("zeros", [P, SUMS], f32)
        unfit_all = sb("unfit_all", [P, 1], f32)
        unfit_n = sb("unfit_n", [P, 1], i32)
        e = sb("e", [P, BATCH, SLOTS], f32)
        e2 = sb("e2", [P, BATCH, SLOTS], f32)
        prob = sb("prob", [P, BATCH, SLOTS], f32)
        weight = sb("weight", [P, BATCH, SLOTS], f32)
        m4 = sb("m4", [P, BATCH], f32)
        r4 = sb("r4", [P, BATCH], f32)
        alone = sb("alone", [P, BATCH], f32)
        w_rec = sb("w_rec", [P, REC], f32)
        w_gathered = sb("w_gathered", [P, MORE, ROW], f32)
        w_index = sb("w_index", [P, MORE + 1], u32)
        w_valid = sb("w_valid", [P, MORE], f32)
        w_tmp = sb("w_tmp", [P, 2, MORE], f32)
        w_score = sb("w_score", [P, MORE + 1], f32)
        w_prob = sb("w_prob", [P, MORE + 1], f32)
        w_x = sb("w_x", [P, F], f32)
        w_first = sb("w_first", [P, F], f32)
        w_m = sb("w_m", [P, 2], f32)
        cols = sb("cols", [P, 4], f32)

        w_flat = w_gathered[:, :, :].rearrange("p k n -> p (k n)")
        key_parts = one_hot[:, :, :, :].rearrange("p a b n -> p (a b n)")[:, 0:2 * BIT_COLS].bitcast(i32
                                                                          ).rearrange("p (a n) -> p a n", a=2)
        key_tmp = w_flat[:, 0:BIT_COLS]
        diff, column, w_t = [w_flat[:, BIT_COLS + k * P:BIT_COLS + (k + 1) * P] for k in range(3)]
        diff, column = diff.bitcast(i32), column.bitcast(i32)

        banks = ctx.enter_context(nc.psum_tensor("banks", [P, 8, 512], f32))
        sums_banks = (5, 1)

        dve_step = sem("dve_step")
        x_loaded = [sem(f"x_loaded{k}") for k in range(len(STAT_GROUPS))]
        w_loaded, iotas, const_made = sem("w_loaded"), sem("iotas"), sem("const_made")
        w_transposed, w_copied, wa_made, w_ready = sem("w_transposed"), sem("w_copied"), sem("wa_made"), sem("w_ready")
        rstd_ready, normed_act, normed_pool, transposed = (
            sem("rstd_ready"), sem("normed_act"), sem("normed_pool"), sem("transposed"))
        relu_ready, projected, rows_ready, sd_ready = sem("relu_ready"), sem("projected"), sem("rows_ready"), sem("sd_ready")
        rows_stored = [sem(f"rows_stored{k}") for k in range(4)]
        r_summed, mean_ready = sem("r_summed"), sem("mean_ready")
        adj_loaded = [sem(f"adj_loaded{u}") for u in range(UNITS)]
        mask_ready, part_packed, words_read = sem("mask_ready"), sem("part_packed"), sem("words_read")
        index_ready = sem("index_ready")
        gathers_done = [sem(f"gathers_done{k}") for k in range(BUFS)]
        out_stored = [sem(f"out_stored{g}") for g in range(GROUPS)]
        logits_ready, exp_ready, out_ready = sem("logits_ready"), sem("exp_ready"), sem("out_ready")
        wide_flagged, prefix_ready, one_hot_ready, records_added = (
            sem("wide_flagged"), sem("prefix_ready"), sem("one_hot_ready"), sem("records_added"))
        sums_added, sums_closed = sem("sums_added"), sem("sums_closed")
        records_closed, records_read = sem("records_closed"), sem("records_read")
        w_index_ready, w_gathers, w_logits, w_exp, w_out_ready, w_stored = (
            sem("w_index_ready"), sem("w_gathers"), sem("w_logits"), sem("w_exp"), sem("w_out_ready"), sem("w_stored"))
        unfit_ready, unfit_summed, verdict = sem("unfit_ready"), sem("unfit_summed"), sem("verdict")
        dn_diag, dn_bcast, dn_adj, dn_x, dn_h, dn_out = (
            sem("dn_diag"), sem("dn_bcast"), sem("dn_adj"), sem("dn_x"), sem("dn_h"), sem("dn_out"))
        dn_row, dn_step, dn_sum, pool_step = sem("dn_row"), sem("dn_step"), sem("dn_sum"), sem("pool_step")
        keys_made, a_loaded = sem("keys_made"), sem("a_loaded")
        dn_max, dn_exp, dn_blk, dn_tr, dn_pt, dn_mm, dn_o = (
            sem("dn_max"), sem("dn_exp"), sem("dn_blk"), sem("dn_tr"), sem("dn_pt"), sem("dn_mm"), sem("dn_o"))

        def tile_of(buffer, t):
            return buffer[:, bass.ds(t, 1), :].rearrange("p a f -> p (a f)")

        block = ctx.enter_context(nc.Block())

        @block.sync
        def _(sp):
            for k, (lo, hi) in enumerate(STAT_GROUPS):
                sp.dma_start(x_all[:, lo:hi, :], x[lo * P:hi * P, :].rearrange("(t p) f -> p t f", p=P)
                             ).then_inc(x_loaded[k], 16)

            def load_unit(i, u):
                sp.dma_start(adj_buf[:, u, :], adj[bass.ds((i * BATCH + u // PARTS) * P, P),
                                                   u % PARTS * PART:(u % PARTS + 1) * PART]).then_inc(adj_loaded[u], 16)

            def load_batch(i, first=0, last=UNITS):
                for u in range(first, last):
                    sp.wait_ge(mask_ready, (i - 1) * UNITS + u + 1)
                    load_unit(i, u)

            def store_batch(i, group):
                sp.wait_ge(out_ready, i + 1)
                sp.dma_start(out[bass.ds(i * (BATCH * P), BATCH * P), :].rearrange("(b p) f -> p b f", p=P),
                             x_all[:, bass.ds(i * BATCH, BATCH), :]).then_inc(out_stored[group], 16)

            for u in range(UNITS):
                load_unit(0, u)
            for k in range(4):
                sp.wait_ge(rows_ready, (k + 1) * (FOURS // 4))
                sp.dma_start(table[k * QUARTER * P:(k + 1) * QUARTER * P, :].rearrange("(t p) n -> p t n", p=P),
                             rows_all[:, k * QUARTER:(k + 1) * QUARTER, :]).then_inc(rows_stored[k], 16)
                if k == 1:
                    load_batch(1, 0, len(EARLY_MASKS))
            load_batch(1, len(EARLY_MASKS), UNITS)
            with sp.Fori(2, STORE_LAG) as i:
                load_batch(i)
            with sp.Fori(STORE_LAG, GROUP_BATCHES + STORE_LAG) as i:
                load_batch(i)
                store_batch(i - STORE_LAG, 0)
            with sp.Fori(GROUP_BATCHES + STORE_LAG, BATCHES) as i:
                load_batch(i)
                store_batch(i - STORE_LAG, 1)
            for i in range(BATCHES - STORE_LAG, BATCHES):
                store_batch(i, 1)

            for g in range(GROUPS):
                sp.wait_ge(out_stored[g], 16 * GROUP_BATCHES)
            sp.wait_ge(w_stored, 16 * GROUPS)
            sp.wait_ge(verdict, 1)
            unfit_nodes = sp.value_load(unfit_n[0:1, 0:1], min_val=0, max_val=N)
            with sp.If(unfit_nodes > 0):
                sp.nop().then_inc(dn_out, 16)
                with sp.Fori(0, TILES) as t:
                    sp.wait_ge(dn_o, t + 1)
                    sp.dma_start(dense_adj, adj[bass.ts(t, P), :]).then_inc(dn_adj, 16)
                    sp.dma_start(x_row, x[bass.ts(t, P), :]).then_inc(dn_x, 16)
                    with sp.Fori(0, TILES // 4) as j:
                        sp.wait_ge(dn_mm, t * (TILES // 4) + j + 1)
                        sp.dma_start(h_blk, table[bass.ts(j, 4 * P), 0:F].rearrange("(b p) f -> p b f", p=P)).then_inc(dn_h, 16)
                    sp.wait_ge(dn_o, t + 2)
                    sp.dma_start(out[bass.ts(t, P), :], o_row).then_inc(dn_out, 16)
                sp.wait_ge(dn_out, 16 * (TILES + 1))

        @block.gpsimd
        def _(pool):
            nc.gpsimd.iota(diff, [[1, P]], base=0, channel_multiplier=-1).then_inc(iotas, 1)
            nc.gpsimd.iota(column, [[1, P]], base=1, channel_multiplier=0).then_inc(iotas, 1)
            nc.gpsimd.iota(node0[:], [[P, BATCH]], base=0, channel_multiplier=1).then_inc(iotas, 1)
            nc.gpsimd.iota(key_parts[:, 0, :], [[0, 2], [1, 256]], base=0, channel_multiplier=0).then_inc(iotas, 1)
            nc.gpsimd.iota(key_parts[:, 1, :], [[1, 2], [0, 256]], base=0, channel_multiplier=0).then_inc(iotas, 1)
            nc.gpsimd.memset(w_x[:], 0.0).then_inc(iotas, 1)
            nc.gpsimd.memset(pool_fence[:], 0.0).then_inc(pool_step, 1)

            def normalize(g, par):
                pool.wait_ge(rstd_ready, g + 1)
                if not among_first_two(g):
                    pool.wait_ge(transposed, g - 1)
                for b in (2, 3):
                    t = g * FOUR + b
                    ins = nc.gpsimd.tensor_scalar(normed[par][:, b], x_all[:, t, :], mv_all[:, t, 0:1], rstd[:, t:t + 1],
                                                  ALU.subtract, ALU.mult)
                ins.then_inc(normed_pool, 1)

            for g in range(FOURS):
                normalize(g, g % 2)
            pool.wait_ge(rows_ready, FOURS)
            nc.gpsimd.tensor_copy(sd_all[:], rows_all[:, :, S_COL:ROW]).then_inc(sd_ready, 1)
            for k in range(4):
                pool.wait_ge(rows_stored[k], 16)
            pool.wait_ge(sd_ready, 1)

            def gather_tile(buf, b):
                for k in range(SLOTS):
                    nc.gpsimd.indirect_dma_start(
                        g_view[buf][:, b, k, :], None, table, bass.IndirectOffsetOnAxis(index[:, buf, b, k:k + 1], 0),
                        bounds_check=N - 1, oob_is_err=False).then_inc(gathers_done[buf], 16)

            def gather_batches(q, first=False, last=False):
                for buf in range(BUFS):
                    i = BUFS * q + buf
                    if not first:
                        pool.wait_ge(out_ready, i - BUFS + 1)
                    pool.wait_ge(index_ready, i + 1)
                    pool.wait_ge(pool_step, i + 1)
                    nc.gpsimd.tensor_tensor(pool_fence[:], pool_fence[:], pool_fence[:], ALU.add).then_inc(pool_step, 1)
                    gather_tile(buf, 0)
                    if last and buf == BUFS - 1:
                        pool.wait_ge(index_ready, i + 2)
                    gather_tile(buf, 1)

            def wide_gather(g):
                pool.wait_ge(w_index_ready, g + 1)
                for k in range(MORE):
                    nc.gpsimd.indirect_dma_start(
                        w_gathered[:, k, :], None, table, bass.IndirectOffsetOnAxis(w_index[:, k:k + 1], 0),
                        bounds_check=N - 1, oob_is_err=False).then_inc(w_gathers, 16)
                nc.gpsimd.indirect_dma_start(
                    w_x[:], None, x, bass.IndirectOffsetOnAxis(w_index[:, MORE:MORE + 1], 0),
                    bounds_check=N - 1, oob_is_err=False).then_inc(w_gathers, 16)

            def wide_store(g):
                pool.wait_ge(out_stored[g], 16 * GROUP_BATCHES)
                pool.wait_ge(w_out_ready, g + 1)
                nc.gpsimd.indirect_dma_start(
                    out, bass.IndirectOffsetOnAxis(w_index[:, MORE:MORE + 1], 0), w_x[:], None,
                    bounds_check=N - 1, oob_is_err=False).then_inc(w_stored, 16)

            gather_batches(0, first=True)
            with pool.Fori(1, GROUP_ROUNDS) as q:
                gather_batches(q)
            wide_gather(0)
            with pool.Fori(GROUP_ROUNDS, ROUNDS - 1) as q:
                gather_batches(q)
            wide_store(0)
            gather_batches(ROUNDS - 1, last=True)
            wide_gather(1)
            wide_store(1)

        @block.scalar
        def _(act):
            act.dma_start(w_ext[:, 0:F], W).then_inc(w_loaded, 16)
            for k in (0, 1):
                act.dma_start(a_sb[:, k:k + 1], a[k * F:(k + 1) * F, :]).then_inc(a_loaded, 16)
            act.wait_ge(w_transposed, 1)
            nc.scalar.copy(w_t, banks[:, 6, 0:P]).then_inc(w_copied, 1)
            act.wait_ge(wa_made, 1)
            nc.scalar.copy(w_ext[:, S_COL:ROW], banks[:, 7, 0:2]).then_inc(w_ready, 1)

            def normalize(g, par):
                act.wait_ge(rstd_ready, g + 1)
                if not among_first_two(g):
                    act.wait_ge(transposed, g - 1)
                for b in (0, 1):
                    t = g * FOUR + b
                    ins = nc.scalar.activation(normed[par][:, b], tile_of(x_all, t), ACT.Identity,
                                               bias=nbias[:, bass.ds(t, 1)], scale=rstd[:, bass.ds(t, 1)])
                ins.then_inc(normed_act, 1)

            def relu_rows(g, par):
                act.wait_ge(transposed, g + 1)
                if not among_first_two(g):
                    act.wait_ge(projected, g - 1)
                nc.scalar.activation(relu_t[par].rearrange("p b f -> p (b f)"), banks[:, par, :], ACT.Relu,
                                     accum_out=r_sums[:, bass.ds(g, 1)]).then_inc(relu_ready, 1)

            def take_rows(g, par):
                act.wait_ge(projected, g + 1)
                nc.scalar.copy(rows_all[:, bass.ds(g * FOUR, FOUR), :].rearrange("p (u w) n -> p u (w n)", u=2),
                               banks[:, 2 + 2 * par:4 + 2 * par, 0:2 * ROW]).then_inc(rows_ready, 1)

            def project(g, par, first=False, last=False):
                if not last:
                    normalize(g + 1, 1 - par)
                relu_rows(g, par)
                if not first:
                    take_rows(g - 1, 1 - par)

            def mask(i, u):
                act.wait_ge(adj_loaded[u], 16 * i + 16)
                if not is_first(i):
                    act.wait_ge(part_packed, (i - 1) * UNITS + u + 1)
                nc.scalar.activation(mask_buf[:, u], adj_buf[:, u], ACT.Sign, bias=minus_half[:]).then_inc(mask_ready, 1)

            normalize(0, 0)
            for g in range(FOURS // 2):
                project(g, g % 2, first=(g == 0))
                if g in EARLY_MASKS:
                    mask(0, EARLY_MASKS.index(g))
            with act.Fori(FOURS // 4, FOURS // 2 - 1) as q:
                for par in (0, 1):
                    project(2 * q + par, par)
            project(FOURS - 2, 0)
            project(FOURS - 1, 1, last=True)
            take_rows(FOURS - 1, 1)

            def softmax(i):
                act.wait_ge(logits_ready, i + 1)
                nc.scalar.activation(prob[:], e2[:], ACT.Exp).then_inc(exp_ready, 1)

            def batch(i, exp=True):
                if not is_first(i):
                    mask(i, 0)
                if exp:
                    softmax(i - 1 - LAG)
                for u in range(len(EARLY_MASKS) if is_first(i) else 1, UNITS):
                    mask(i, u)

            def wide_softmax(g):
                act.wait_ge(w_logits, g + 1)
                nc.scalar.activation(w_prob[:], w_score[:], ACT.Exp, bias=w_m[:, 0:1]).then_inc(w_exp, 1)

            for i in range(1 + LAG):
                batch(i, exp=False)
            with act.Fori(1 + LAG, GROUP_BATCHES + 1 + BUFS) as i:
                batch(i)
            wide_softmax(0)
            with act.Fori(GROUP_BATCHES + 1 + BUFS, BATCHES) as i:
                batch(i)
            for i in range(BATCHES - 1 - LAG, BATCHES):
                softmax(i)
            wide_softmax(1)

            act.wait_ge(verdict, 1)
            unfit_nodes = act.value_load(unfit_n[0:1, 0:1], min_val=0, max_val=N)
            with act.If(unfit_nodes > 0):
                act.nop().then_inc(dn_pt, 1)
                with act.Fori(0, TILES) as t:
                    act.wait_ge(dn_max, t + 1)
                    nc.scalar.activation(dense_e, dense_e, ACT.Exp, bias=cols[:, 0:1], accum_out=cols[:, 1:2]
                                         ).then_inc(dn_exp, 1)
                    act.wait_ge(dn_exp, t + 1)
                    with act.Fori(0, TILES // 4) as j:
                        act.wait_ge(dn_tr, t * (TILES // 4) + j + 1)
                        nc.scalar.copy(e_blk, dense_e[:, bass.ds(j * (4 * P), 4 * P)].rearrange("p (b f) -> p b f", b=4)
                                       ).then_inc(dn_blk, 1)
                        act.wait_ge(dn_tr, t * (TILES // 4) + j + 2)
                        act.wait_ge(dn_mm, t * (TILES // 4) + j + 1)
                        nc.scalar.copy(p_t, banks[:, 4, :].rearrange("p (b f) -> p b f", b=4)).then_inc(dn_pt, 1)

        @block.vector
        def _(dve):
            done = Count(dve_step)

            def settled():
                dve.wait_ge(dve_step, done.value())

            def fenced():
                settled()
                done.add(nc.vector.memset(fence[:], 0.0))

            v = nc.vector
            done.add(v.memset(ones[:], 1.0))
            done.add(v.memset(ones_b[:], 1.0))
            done.add(v.memset(zeros[:], 0.0))
            done.add(v.memset(wide_base[:], 1.0))
            done.add(v.memset(node_base[:], 0.0))
            done.add(v.memset(unfit_all[:], 0.0))
            done.add(v.memset(minus_half[:], -0.5))
            dve.wait_ge(iotas, 6)
            done.add(v.tensor_scalar(ident[:], diff, 0.0, None, ALU.is_equal))
            done.add(v.tensor_scalar(before[:], diff, 0.0, None, ALU.is_gt))
            done.add(v.tensor_copy(column_1[:], column))
            settled()
            v.memset(rec[:], 1.0).then_inc(const_made, 1)

            def statistics(k):
                lo, hi = STAT_GROUPS[k]
                dve.wait_ge(x_loaded[k], 16)
                settled()
                for t in range(lo, hi):
                    done.add(v.bn_stats(stats[:, t - lo], x_all[:, t, :]))
                settled()
                for t in range(lo, hi):
                    done.add(v.bn_aggr(mv_all[:, t, :], stats[:, t - lo]))
                settled()
                done.add(v.tensor_scalar(var_e[:, lo:hi], mv_all[:, lo:hi, 1], EPS, None, ALU.add))
                settled()
                square, factor = newton[:, 0, 0:hi - lo], newton[:, 1, 0:hi - lo]
                done.add(v.tensor_scalar(square.bitcast(i32), var_e[:, lo:hi].bitcast(i32), 1, None, ALU.arith_shift_right))
                settled()
                done.add(v.tensor_scalar(rstd[:, lo:hi].bitcast(i32), square.bitcast(i32), -1.0, float(MAGIC),
                                         ALU.mult, ALU.add))
                for _ in range(NEWTON_STEPS):
                    settled()
                    done.add(v.tensor_tensor(square, rstd[:, lo:hi], rstd[:, lo:hi], ALU.mult))
                    settled()
                    done.add(v.scalar_tensor_tensor(factor, square, -0.5, var_e[:, lo:hi], ALU.mult, ALU.mult))
                    settled()
                    done.add(v.scalar_tensor_tensor(rstd[:, lo:hi], factor, 1.5, rstd[:, lo:hi], ALU.add, ALU.mult))
                settled()
                v.scalar_tensor_tensor(nbias[:, lo:hi], mv_all[:, lo:hi, 0], -1.0, rstd[:, lo:hi], ALU.mult, ALU.mult
                                       ).then_inc(rstd_ready, (hi - lo) // FOUR)

            for k in range(len(STAT_GROUPS)):
                statistics(k)

            for c in range(BITS):
                done.add(v.tensor_scalar(bit_ident[:, c], ident[:], float(1 << c) / 2, None, ALU.mult))
            done.add(v.tensor_scalar(key_tmp, key_parts[:, 0], ident[:, 0:1], 1.0 / BIT_COLS, ALU.mult, ALU.mult))
            settled()
            done.add(v.tensor_scalar(rest[:], key_parts[:, 1], ident[:, 1:2], 256.0 / BIT_COLS, ALU.mult, ALU.mult))
            settled()
            done.add(v.tensor_tensor(key_tmp, key_tmp, rest[:], ALU.add))
            settled()
            done.add(v.tensor_scalar(fence[:], ident[:, 2:3], -0.5, None, ALU.mult))
            settled()
            v.tensor_scalar(key_rows[:], key_tmp, fence[:, 0:1], None, ALU.add).then_inc(keys_made, 1)
            dve.wait_ge(relu_ready, FOURS)
            done.add(v.tensor_reduce(r_sum[:], r_sums[:], AX.X, ALU.add))
            settled()
            v.tensor_scalar(r_sum_cols[:], ones[:], r_sum[:, 0:1], None, ALU.mult).then_inc(r_summed, 1)
            dve.wait_ge(mean_ready, 1)
            done.add(v.tensor_scalar(mean_h[:], banks[:, 0, 0:F], 1.0 / N, None, ALU.mult))
            dve.wait_ge(keys_made, 1)
            dve.wait_ge(w_ready, 1)
            done.add(v.memset(w_gathered[:], 0.0))
            dve.wait_ge(sd_ready, 1)

            def first_words(b):
                done.add(v.max(words[:, b, 0:8], banks[:, 6 + b]))

            def remove_words(b):
                v.match_replace(rest[:], words[:, b, 0:8], banks[:, 6 + b], -float(1 << BITS)).then_inc(words_read, 1)

            def second_words(b):
                done.add(v.max(words[:, b, 8:16], rest[:]))

            def decode(par, lo=0, hi=BATCH):
                B = slice(lo, hi)
                done.add(v.tensor_scalar(wi[0][:, B], words[:, B], float(BIT_COLS), None, ALU.mult))
                settled()
                done.add(v.tensor_scalar(wi[1][:, B], wi[0][:, B], BIT_COLS - 1, None, ALU.bitwise_and))
                done.add(v.tensor_scalar(wi[2][:, B], wi[0][:, B], 9, None, ALU.arith_shift_right))
                settled()
                done.add(v.tensor_scalar(wf[0][:, B], wi[2][:, B], float(1 << (BITS - 1)), None, ALU.add))
                settled()
                done.add(v.tensor_scalar(wi[0][:, B], wf[0][:, B].bitcast(i32), 23, None, ALU.logical_shift_right))
                done.add(v.tensor_scalar(top_bit[:, B], wf[0][:, B].bitcast(i32), 0x7F800000, None, ALU.bitwise_and))
                settled()
                done.add(v.scalar_tensor_tensor(cand[:, B, 0:WIDE], wi[0][:, B], float(BIT_COLS), wi[1][:, B], ALU.mult, ALU.add))
                done.add(v.tensor_tensor(wf[1][:, B], wf[0][:, B], top_bit[:, B].bitcast(f32), ALU.subtract))
                settled()
                done.add(v.tensor_scalar(wi[2][:, B], wf[1][:, B].bitcast(i32), 23, None, ALU.logical_shift_right))
                done.add(v.tensor_scalar(top_bit[:, B], wf[1][:, B].bitcast(i32), 0x7F800000, None, ALU.bitwise_and))
                settled()
                done.add(v.scalar_tensor_tensor(cand[:, B, WIDE:], wi[2][:, B], float(BIT_COLS), wi[1][:, B], ALU.mult, ALU.add))
                done.add(v.tensor_tensor(wf[2][:, B], wf[1][:, B], top_bit[:, B].bitcast(f32), ALU.subtract))
                fenced()
                for b in range(lo, hi):
                    done.add(v.max(top[:, b, 0:8], cand[:, b]))
                settled()
                done.add(v.tensor_scalar(skip[:, B], top[:, B, 0:SLOTS], float(EXP_BIAS), SKIP, ALU.is_lt, ALU.mult))
                done.add(v.tensor_scalar(valid[:, par, B], top[:, B, 0:SLOTS], float(EXP_BIAS), None, ALU.is_ge))
                settled()
                v.scalar_tensor_tensor(index[:, par, B], top[:, B, 0:SLOTS], -float(EXP_BIAS), skip[:, B],
                                       ALU.add, ALU.add).then_inc(index_ready, 1)
                done.add(v.tensor_scalar(masked[:, par, B], valid[:, par, B], 1.0, MASKED, ALU.subtract, ALU.mult))
                done.add(v.tensor_reduce(unfit[:, 0, B], wf[2][:, B], AX.X, ALU.max))
                done.add(v.tensor_copy(unfit[:, 1, B], wf[0][:, B, WIDE - 1]))
                done.add(v.tensor_scalar(cand_half[:, B], cand[:, B], float(EXP_BIAS), 0.5, ALU.is_ge, ALU.subtract))
                settled()
                done.add(v.tensor_reduce(unfit[:, 2, B], cand_half[:, B], AX.X, ALU.add))
                for b in range(lo, hi):
                    done.add(v.match_replace(cand[:, b], top[:, b, 0:8], cand[:, b], 0.0))
                fenced()
                for b in range(lo, hi):
                    done.add(v.max(top[:, b, 8:16], cand[:, b]))
                settled()

            def make_records(i):
                if not is_first(i):
                    dve.wait_ge(records_added, i)
                done.add(v.tensor_copy(rec[:, :, 0:MORE], top[:, :, SLOTS:]))
                done.add(v.tensor_copy(rec[:, :, REC_S], sd_all[:, bass.ds(i * BATCH, BATCH), 0]))
                done.add(v.tensor_scalar(rec[:, :, REC_NODE], node0[:], node_base[:, 0:1], None, ALU.add))
                settled()
                done.add(v.tensor_scalar(node_base[:], node_base[:], float(BATCH * P), None, ALU.add))
                v.tensor_scalar(is_wide[:], top[:, :, SLOTS], float(EXP_BIAS), None, ALU.is_ge).then_inc(wide_flagged, 1)

            def place_wide(i, par):
                dve.wait_ge(prefix_ready, i + 1)
                done.add(v.scalar_tensor_tensor(pos[:], banks[:, 2, 0:BATCH], wide_base[:, 0:1], is_wide[:], ALU.add, ALU.mult))
                settled()
                done.add(v.tensor_tensor(wide_base[:], wide_base[:], banks[:, 2, BATCH:BATCH + 1], ALU.add))
                done.add(v.tensor_scalar(unfit[:, 3], pos[:], float(P), None, ALU.subtract))
                if not (isinstance(i, int) and i < BUFS):
                    dve.wait_ge(sums_added, i - BUFS + 1)
                for b in range(BATCH):
                    ins = v.tensor_scalar(one_hot[:, par, b], column_1[:], pos[:, b:b + 1], None, ALU.is_equal)
                ins.then_inc(one_hot_ready, 1)
                settled()
                done.add(v.tensor_reduce(unfit_top[:], unfit[:], AX.XY, ALU.max))
                settled()
                done.add(v.tensor_tensor(unfit_all[:], unfit_all[:], unfit_top[:], ALU.max))

            def logits(i, par, gathered_times):
                d = g_view[par][:, :, :, D_COL]
                s = sd_all[:, bass.ds(i * BATCH, BATCH), 0:1].to_broadcast([P, BATCH, SLOTS])
                dve.wait_ge(gathers_done[par], 16 * BATCH * SLOTS * gathered_times)
                settled()
                done.add(v.tensor_tensor(e[:], d, s, ALU.add))
                settled()
                done.add(v.scalar_tensor_tensor(e2[:], e[:], ALPHA, e[:], ALU.mult, ALU.max))
                settled()
                done.add(v.tensor_tensor(e[:], e2[:], valid[:, par], ALU.mult))
                settled()
                done.add(v.tensor_tensor(e[:], e[:], masked[:, par], ALU.add))
                settled()
                done.add(v.tensor_reduce(max_sum[:, par, :, 0], e[:], AX.X, ALU.max))
                settled()
                v.tensor_tensor(e2[:], e[:], max_sum[:, par, :, 0:1].to_broadcast([P, BATCH, SLOTS]), ALU.subtract
                                ).then_inc(logits_ready, 1)

            def weighted_sum(i, par, gathered_times):
                dve.wait_ge(exp_ready, i + 1)
                done.add(v.tensor_tensor(weight[:], prob[:], valid[:, par], ALU.mult))
                settled()
                l4 = max_sum[:, par, :, 1]
                done.add(v.tensor_reduce(l4, weight[:], AX.X, ALU.add))
                settled()
                done.add(v.tensor_scalar(alone[:], l4, 0.5, None, ALU.is_lt))
                done.add(v.tensor_scalar(m4[:], l4, 0.5, None, ALU.max))
                settled()
                done.add(v.reciprocal(r4[:], m4[:]))
                settled()
                done.add(v.tensor_tensor(weight[:], weight[:], r4[:].unsqueeze(2).to_broadcast([P, BATCH, SLOTS]), ALU.mult))
                at = [tile_of(x_all, i * BATCH + b) for b in range(BATCH)]
                for b in range(BATCH):
                    done.add(v.scalar_tensor_tensor(at[b], mean_h[:], alone[:, b:b + 1], at[b], ALU.mult, ALU.add))
                for k in range(SLOTS):
                    settled()
                    for b in range(BATCH):
                        ins = v.scalar_tensor_tensor(at[b], g_view[par][:, b, k, 0:F], weight[:, b, k:k + 1], at[b],
                                                     ALU.mult, ALU.add)
                        if k < SLOTS - 1 or b < BATCH - 1:
                            done.add(ins)
                ins.then_inc(out_ready, 1)

            def step(q, buf, lagging):
                i = BUFS * q + buf
                dve.wait_ge(part_packed, i * UNITS + PARTS)
                fenced()
                first_words(0)
                if lagging:
                    logits(i - LAG, (buf - LAG) % BUFS, q + (buf >= LAG))
                fenced()
                remove_words(0)
                dve.wait_ge(words_read, i * BATCH + 1)
                dve.wait_ge(part_packed, i * UNITS + UNITS)
                fenced()
                second_words(0)
                first_words(1)
                fenced()
                remove_words(1)
                dve.wait_ge(words_read, i * BATCH + 2)
                fenced()
                second_words(1)
                settled()
                decode(buf)
                make_records(i)
                if lagging:
                    weighted_sum(i - LAG, (buf - LAG) % BUFS, q + (buf >= LAG))
                place_wide(i, buf)

            def last_step(i):
                dve.wait_ge(part_packed, i * UNITS + PARTS)
                fenced()
                first_words(0)
                fenced()
                remove_words(0)
                dve.wait_ge(words_read, i * BATCH + 1)
                fenced()
                second_words(0)
                settled()
                decode(i % BUFS, 0, 1)
                logits(i - LAG, (i - LAG) % BUFS, (i - LAG) // BUFS + 1)
                dve.wait_ge(part_packed, i * UNITS + UNITS)
                fenced()
                first_words(1)
                fenced()
                remove_words(1)
                dve.wait_ge(words_read, i * BATCH + 2)
                fenced()
                second_words(1)
                settled()
                decode(i % BUFS, 1, 2)
                make_records(i)
                place_wide(i, i % BUFS)
                weighted_sum(i - LAG, (i - LAG) % BUFS, (i - LAG) // BUFS + 1)

            def main_round(q, first=False):
                for buf in range(BUFS):
                    step(q, buf, not (first and buf < LAG))

            def wide_index(g):
                dve.wait_ge(records_closed, g + 1)
                if g:
                    dve.wait_ge(w_stored, 16 * g)
                settled()
                v.tensor_copy(w_rec[:], banks[:, 3, 0:REC]).then_inc(records_read, 1)
                dve.wait_ge(records_read, g + 1)
                done.add(v.tensor_scalar(w_tmp[:, 0], w_rec[:, 0:MORE], float(EXP_BIAS), SKIP, ALU.is_lt, ALU.mult))
                done.add(v.tensor_scalar(w_valid[:], w_rec[:, 0:MORE], float(EXP_BIAS), None, ALU.is_ge))
                done.add(v.tensor_scalar(w_m[:, 0:1], w_rec[:, REC_ONE:REC_ONE + 1], -SKIP, SKIP, ALU.mult, ALU.add))
                settled()
                done.add(v.scalar_tensor_tensor(w_index[:, 0:MORE], w_rec[:, 0:MORE], -float(EXP_BIAS), w_tmp[:, 0],
                                                ALU.add, ALU.add))
                settled()
                v.tensor_tensor(w_index[:, MORE:MORE + 1], w_rec[:, REC_NODE:REC_NODE + 1], w_m[:, 0:1], ALU.add
                                ).then_inc(w_index_ready, 1)

            def wide_sum(g):
                dve.wait_ge(w_gathers, 16 * (MORE + 1) * (g + 1))
                settled()
                done.add(v.tensor_scalar(w_tmp[:, 0], w_gathered[:, :, D_COL], w_rec[:, REC_S:REC_S + 1], None, ALU.add))
                settled()
                done.add(v.scalar_tensor_tensor(w_tmp[:, 1], w_tmp[:, 0], ALPHA, w_tmp[:, 0], ALU.mult, ALU.max))
                settled()
                done.add(v.tensor_tensor(w_tmp[:, 0], w_tmp[:, 1], w_valid[:], ALU.mult))
                settled()
                done.add(v.tensor_scalar(w_tmp[:, 1], w_valid[:], 1.0, MASKED, ALU.subtract, ALU.mult))
                settled()
                done.add(v.tensor_tensor(w_score[:, 0:MORE], w_tmp[:, 0], w_tmp[:, 1], ALU.add))
                settled()
                dve.wait_ge(sums_closed, g + 1)
                sums = banks[:, sums_banks[g], 0:SUMS]
                done.add(v.tensor_copy(w_score[:, MORE:MORE + 1], sums[:, F:F + 1]))
                settled()
                v.tensor_reduce(w_m[:, 0:1], w_score[:], AX.X, ALU.max, negate=True).then_inc(w_logits, 1)
                done.add(v.scalar_tensor_tensor(w_first[:], w_x[:], -1.0, sums[:, 0:F], ALU.mult, ALU.add))
                dve.wait_ge(w_exp, g + 1)
                settled()
                done.add(v.tensor_tensor(w_prob[:, MORE:MORE + 1], w_prob[:, MORE:MORE + 1], sums[:, F + 1:F + 2], ALU.mult))
                settled()
                done.add(v.tensor_reduce(w_m[:, 1:2], w_prob[:], AX.X, ALU.add))
                settled()
                done.add(v.tensor_scalar(w_m[:, 0:1], w_m[:, 1:2], 0.5, None, ALU.max))
                settled()
                done.add(v.reciprocal(w_m[:, 1:2], w_m[:, 0:1]))
                settled()
                done.add(v.tensor_scalar(w_prob[:], w_prob[:], w_m[:, 1:2], None, ALU.mult))
                settled()
                done.add(v.tensor_scalar(w_first[:], w_first[:], w_prob[:, MORE:MORE + 1], None, ALU.mult))
                for k in range(0, MORE, 2):
                    settled()
                    for j, part in ((k, w_x), (k + 1, w_first)):
                        done.add(v.scalar_tensor_tensor(part[:], w_gathered[:, j, 0:F], w_prob[:, j:j + 1], part[:],
                                                        ALU.mult, ALU.add))
                settled()
                v.tensor_tensor(w_x[:], w_x[:], w_first[:], ALU.add).then_inc(w_out_ready, 1)

            def main_rounds(lo, hi):
                with dve.Fori(lo, hi) as q:
                    done.enter(q - lo, BUFS * DVE_STEPS)
                    main_round(q)
                    done.leave(hi - lo)

            main_round(0, first=True)
            main_rounds(1, GROUP_ROUNDS)
            wide_index(0)
            done.add(v.memset(wide_base[:], 1.0))
            main_round(GROUP_ROUNDS)
            wide_sum(0)
            main_rounds(GROUP_ROUNDS + 1, ROUNDS - 1)
            for buf in range(BUFS - 1):
                step(ROUNDS - 1, buf, True)
            last_step(BATCHES - 1)
            wide_index(1)
            for i in range(BATCHES - LAG, BATCHES):
                logits(i, i % BUFS, ROUNDS)
                weighted_sum(i, i % BUFS, ROUNDS)
            wide_sum(1)

            settled()
            v.tensor_scalar(unfit_top[:], unfit_all[:], 0.0, None, ALU.is_gt).then_inc(unfit_ready, 1)
            dve.wait_ge(unfit_summed, 1)
            v.tensor_copy(unfit_n[:], banks[:, 4, 0:1]).then_inc(verdict, 1)
            dve.wait_ge(verdict, 1)
            unfit_nodes = dve.value_load(unfit_n[0:1, 0:1], min_val=0, max_val=N)
            with dve.If(unfit_nodes > 0):
                dve.nop().then_inc(dn_row, 1)
                dve.nop().then_inc(dn_o, 1)
                dve.nop().then_inc(dn_step, 1)
                with dve.Fori(0, TILES) as j:
                    dve.wait_ge(dn_bcast, j + 1)
                    v.tensor_scalar(d_diag, ident[:], sd_all[:, j, 1:2], None, ALU.mult).then_inc(dn_diag, 1)
                    dve.wait_ge(dn_bcast, j + 2)
                    v.tensor_copy(dense_d[:, bass.ds(j * P, P)], banks[:, 4, 0:P]).then_inc(dn_row, 1)
                dve.wait_ge(dn_row, TILES + 1)
                v.memset(d_diag, 0.0).then_inc(dn_row, 1)
                with dve.Fori(0, TILES) as t:
                    dense = Count(dn_step, credit=1)
                    dense.enter(t, 8)

                    def dense_settled():
                        dve.wait_ge(dn_step, dense.value())

                    dve.wait_ge(dn_adj, 16 * t + 16)
                    dve.wait_ge(dn_tr, t * (TILES // 4) + 1)
                    dense.add(v.tensor_scalar(dense_e, dense_d, sd_all[:, t, 0:1], None, ALU.add))
                    dense.add(v.tensor_scalar(dense_m, dense_adj, 0.0, None, ALU.is_gt))
                    dense_settled()
                    dense.add(v.scalar_tensor_tensor(dense_e, dense_e, ALPHA, dense_e, ALU.mult, ALU.max))
                    dense_settled()
                    dense.add(v.tensor_tensor(dense_e, dense_e, dense_m, ALU.mult))
                    dense_settled()
                    dense.add(v.tensor_scalar(dense_m, dense_m, 1.0, MASKED, ALU.subtract, ALU.mult))
                    dense_settled()
                    dense.add(v.tensor_tensor(dense_e, dense_e, dense_m, ALU.add))
                    dense_settled()
                    v.tensor_reduce(cols[:, 0:1], dense_e, AX.X, ALU.max, negate=True).then_inc(dn_max, 1)
                    dve.wait_ge(dn_exp, t + 1)
                    dense.add(v.reciprocal(cols[:, 2:3], cols[:, 1:2]))
                    dense_settled()
                    dve.wait_ge(dn_sum, t + 1)
                    dve.wait_ge(dn_x, 16 * t + 16)
                    dve.wait_ge(dn_out, 16 * t + 16)
                    v.scalar_tensor_tensor(o_row, banks[:, 5, 0:F], cols[:, 2:3], x_row, ALU.mult, ALU.add).then_inc(dn_o, 1)
                    dense.add(v.memset(fence[:], 0.0))

        @block.tensor
        def _(pe):
            mm = nc.tensor.matmul
            pe.wait_ge(const_made, 1)
            pe.wait_ge(w_loaded, 16)
            nc.tensor.transpose(banks[:, 6, 0:P], w_ext[:, 0:F], ident[:]).then_inc(w_transposed, 1)
            pe.wait_ge(w_copied, 1)
            pe.wait_ge(a_loaded, 32)
            mm(banks[:, 7, 0:2], w_t, a_sb[:], start=True, stop=True).then_inc(wa_made, 1)
            pe.wait_ge(w_ready, 1)

            def transpose_rows(g, par):
                pe.wait_ge(normed_act, g + 1)
                pe.wait_ge(normed_pool, g + 1)
                if not among_first_two(g):
                    pe.wait_ge(relu_ready, g - 1)
                for b in range(FOUR):
                    ins = nc.tensor.transpose(banks[:, par, b * P:(b + 1) * P], normed[par][:, b], ident[:])
                ins.then_inc(transposed, 1)

            def project(g, par):
                pe.wait_ge(relu_ready, g + 1)
                if not among_first_two(g):
                    pe.wait_ge(rows_ready, g - 1)
                for b in range(FOUR):
                    at = b % 2 * ROW
                    ins = mm(banks[:, 2 + 2 * par + b // 2, at:at + ROW], relu_t[par][:, b], w_ext[:], start=True, stop=True)
                ins.then_inc(projected, 1)

            def project_pair(q, last=False):
                transpose_rows(2 * q + 1, 1)
                project(2 * q, 0)
                if not last:
                    transpose_rows(2 * q + 2, 0)
                project(2 * q + 1, 1)

            transpose_rows(0, 0)
            project_pair(0)
            with pe.Fori(1, FOURS // 2 - 1) as q:
                project_pair(q)
            project_pair(FOURS // 2 - 1, last=True)
            pe.wait_ge(r_summed, 1)
            mm(banks[:, 0, 0:F], r_sum_cols[:], w_ext[:, 0:F], start=True, stop=True).then_inc(mean_ready, 1)
            pe.wait_ge(rows_ready, FOURS)
            pe.wait_ge(keys_made, 1)

            def pack(i, u):
                b, h = u // PARTS, u % PARTS
                pe.wait_ge(mask_ready, i * UNITS + u + 1)
                if h == 0:
                    if not is_first(i):
                        pe.wait_ge(words_read, (i - 1) * BATCH + b + 1)
                    mm(banks[:, 6 + b], ones_b[0:3, :], key_rows[0:3, :], start=True, stop=False)
                for c in range(PART_BITS):
                    ins = mm(banks[:, 6 + b], bit_ident[:, h * PART_BITS + c], mask_buf[:, u, c * BIT_COLS:(c + 1) * BIT_COLS],
                             start=False, stop=(h == PARTS - 1 and c == PART_BITS - 1))
                ins.then_inc(part_packed, 1)

            def count_wide(i):
                pe.wait_ge(wide_flagged, i + 1)
                if not is_first(i):
                    pe.wait_ge(one_hot_ready, i)
                for b in range(BATCH):
                    mm(banks[:, 2, b:b + 1], before[:], is_wide[:, b:b + 1], start=True, stop=(b == 0))
                    for c in range(b):
                        mm(banks[:, 2, b:b + 1], ones_b[:], is_wide[:, c:c + 1], start=False, stop=(c == b - 1))
                for b in range(BATCH):
                    ins = mm(banks[:, 2, BATCH:BATCH + 1], ones_b[:], is_wide[:, b:b + 1], start=(b == 0), stop=(b == BATCH - 1))
                ins.then_inc(prefix_ready, 1)

            def add_records(i, par):
                pe.wait_ge(one_hot_ready, i + 1)
                for b in range(BATCH):
                    ins = mm(banks[:, 3, 0:REC], one_hot[:, par, b], rec[:, b], start=False, stop=False)
                ins.then_inc(records_added, 1)

            def add_sums(i, par, group):
                pe.wait_ge(out_ready, i + 1)
                bank = sums_banks[group]
                for b in range(BATCH):
                    tile_out = tile_of(x_all, i * BATCH + b)
                    mm(banks[:, bank, 0:F], one_hot[:, par, b], tile_out, start=False, stop=False)
                    ins = mm(banks[:, bank, F:SUMS], one_hot[:, par, b], max_sum[:, par, b], start=False, stop=False)
                ins.then_inc(sums_added, 1)

            def batch(i, buf, sums_of=None):
                pack(i, 0)
                count_wide(i - 1)
                for u in range(1, UNITS):
                    pack(i, u)
                add_records(i - 1, (buf - 1) % BUFS)
                if sums_of is not None:
                    add_sums(i - 1 - LAG, (buf - 1 - LAG) % BUFS, sums_of)

            def main_rounds(lo, hi, group):
                with pe.Fori(lo, hi) as q:
                    for buf in range(BUFS):
                        batch(BUFS * q + buf, buf, group)

            def add_zeros(region, start, stop):
                return mm(region, ones[:], zeros[:, 0:region.shape[1]], start=start, stop=stop)

            records = banks[:, 3, 0:REC]
            sums = [banks[:, bank, 0:SUMS] for bank in sums_banks]

            for u in range(UNITS):
                pack(0, u)
            add_zeros(records, start=True, stop=False)
            for group in range(GROUPS):
                add_zeros(sums[group], start=True, stop=False)
            for i in range(1, BUFS):
                batch(i, i, 0 if i > LAG else None)
            main_rounds(1, GROUP_ROUNDS, 0)
            i = GROUP_BATCHES
            pack(i, 0)
            count_wide(i - 1)
            add_records(i - 1, (i - 1) % BUFS)
            add_zeros(records, start=False, stop=True).then_inc(records_closed, 1)
            add_sums(i - 1 - LAG, (i - 1 - LAG) % BUFS, 0)
            for u in range(1, UNITS):
                pack(i, u)
            pe.wait_ge(records_read, 1)
            add_zeros(records, start=True, stop=False)
            for i in range(GROUP_BATCHES + 1, GROUP_BATCHES + BUFS):
                batch(i, i % BUFS, 0 if i - 1 - LAG < GROUP_BATCHES else 1)
                if i - 1 - LAG == GROUP_BATCHES - 1:
                    add_zeros(sums[0], start=False, stop=True).then_inc(sums_closed, 1)
            main_rounds(GROUP_ROUNDS + 1, ROUNDS, 1)
            count_wide(BATCHES - 1)
            add_records(BATCHES - 1, BUFS - 1)
            add_zeros(records, start=False, stop=True).then_inc(records_closed, 1)
            for i in range(BATCHES - 1 - LAG, BATCHES):
                add_sums(i, i % BUFS, 1)
            add_zeros(sums[1], start=False, stop=True).then_inc(sums_closed, 1)
            pe.wait_ge(unfit_ready, 1)
            mm(banks[:, 4, 0:1], ones[:], unfit_top[:], start=True, stop=True).then_inc(unfit_summed, 1)

            pe.wait_ge(verdict, 1)
            unfit_nodes = pe.value_load(unfit_n[0:1, 0:1], min_val=0, max_val=N)
            with pe.If(unfit_nodes > 0):
                pe.nop().then_inc(dn_bcast, 1)
                pe.nop().then_inc(dn_tr, 1)
                pe.nop().then_inc(dn_mm, 1)
                with pe.Fori(0, TILES) as j:
                    pe.wait_ge(dn_diag, j + 1)
                    pe.wait_ge(dn_row, j + 1)
                    mm(banks[:, 4, 0:P], ones[:], d_diag, start=True, stop=True).then_inc(dn_bcast, 1)
                pe.wait_ge(dn_row, TILES + 2)
                with pe.Fori(0, TILES) as t:
                    pe.wait_ge(dn_o, t + 1)
                    mm(banks[:, 5, 0:F], ones[:], d_diag, start=True, stop=False)
                    with pe.Fori(0, TILES // 4) as j:
                        at = t * (TILES // 4) + j
                        pe.wait_ge(dn_blk, at + 1)
                        pe.wait_ge(dn_pt, at + 1)
                        for b in range(4):
                            ins = nc.tensor.transpose(banks[:, 4, b * P:(b + 1) * P], e_blk[:, b], ident[:])
                        ins.then_inc(dn_tr, 1)
                        pe.wait_ge(dn_pt, at + 2)
                        pe.wait_ge(dn_h, 16 * at + 16)
                        for b in range(4):
                            ins = mm(banks[:, 5, 0:F], p_t[:, b], h_blk[:, b], start=False, stop=False)
                        ins.then_inc(dn_mm, 1)
                    mm(banks[:, 5, 0:F], ones[:], d_diag, start=False, stop=True).then_inc(dn_sum, 1)


def among_first_two(g):
    return isinstance(g, int) and g < 2


def is_first(i):
    return isinstance(i, int) and i == 0


def kernel(**inputs):
    import numpy as np
    import concourse.bacc as bacc
    from concourse.bass_utils import run_bass_kernel_spmd

    nc = bacc.Bacc("TRN2", target_bir_lowering=False, num_devices=1)
    arrays, args = {}, []
    for name in ("x", "adj", "L0_gnn_W", "L0_gnn_a"):
        arrays[f"in_{name}"] = np.ascontiguousarray(inputs[name])
        args.append(nc.dram_tensor(f"in_{name}", arrays[f"in_{name}"].shape,
                                   mybir.dt.from_np(arrays[f"in_{name}"].dtype), kind="ExternalInput").ap())
    args.append(nc.dram_tensor("out", (N, F), mybir.dt.float32, kind="ExternalOutput").ap())
    gat_kernel(nc, *args)
    return run_bass_kernel_spmd(nc, [arrays], core_ids=[0]).results[0]["out"]
```
